# Optimizing a Trainium2 kernel written in Bass

```python
import numpy as np
import jax
import jax.numpy as jnp

def _softmax(x, axis=-1):
    return jax.nn.softmax(x, axis=axis)

def _gelu(x):
    return jax.nn.gelu(x, approximate=True)

def _silu(x):
    return jax.nn.silu(x)

def _sigmoid(x):
    return jax.nn.sigmoid(x)

def _layernorm(x, axis=-1, eps=1e-05):
    m = jnp.mean(x, axis=axis, keepdims=True)
    v = jnp.var(x, axis=axis, keepdims=True)
    return (x - m) / jnp.sqrt(v + eps)

def _scatter_add(tgt, idx, src, axis=0):
    return tgt.at[idx].add(src)

def _segment_sum(src, seg, n):
    return jax.ops.segment_sum(src, seg, n)
kernel_name = 'mk_seq_postln_d1_jaxref_r4_386a6e'

def setup_inputs(seed: int=0):
    np.random.seed(seed)
    _w = jnp.asarray

    def _L0_attn_setup():
        import jax, jax.numpy as jnp
        import numpy as np
        B, N, D = (2, 1024, 512)
        H, DH, W = (8, 128, 128)
        SCALE = 8.0

        def _l2norm(t):
            return t / jnp.maximum(jnp.linalg.norm(t, axis=-1, keepdims=True), 1e-12)
        key = jax.random.key(seed)
        ks = jax.random.split(key, 5)
        return {'x': jax.random.normal(ks[0], (B, N, D), jnp.float32), 'Wq': jax.random.normal(ks[1], (H * DH, D), jnp.float32) * 0.02, 'Wkv': jax.random.normal(ks[2], (2 * H * DH, D), jnp.float32) * 0.02, 'q_scale': jnp.ones((DH,), jnp.float32), 'k_scale': jnp.ones((DH,), jnp.float32), 'Wg': jax.random.normal(ks[3], (H, D), jnp.float32) * 0.02, 'bg': jnp.zeros((H,), jnp.float32), 'Wo': jax.random.normal(ks[4], (D, H * DH), jnp.float32) * 0.02}
    _L0_attn_in = _L0_attn_setup()

    def _L0_ffn_setup():
        import jax, jax.numpy as jnp
        import numpy as np
        B, S, DIM = (2, 512, 512)
        INTER = 256
        E = 8
        K = 2
        N_SHARED = 1
        ROUTE_SCALE = 1.0
        key = jax.random.key(seed)
        ks = jax.random.split(key, 8)
        s_in = 1.0 / np.sqrt(DIM)
        s_hid = 1.0 / np.sqrt(INTER)
        return {'x': jax.random.normal(ks[0], (B, S, DIM), dtype=jnp.float32), 'gate_w': jax.random.normal(ks[1], (E, DIM), dtype=jnp.float32) * s_in, 'w1': jax.random.normal(ks[2], (E, INTER, DIM), dtype=jnp.float32) * s_in, 'w2': jax.random.normal(ks[3], (E, DIM, INTER), dtype=jnp.float32) * s_hid, 'w3': jax.random.normal(ks[4], (E, INTER, DIM), dtype=jnp.float32) * s_in, 'ws1': jax.random.normal(ks[5], (N_SHARED * INTER, DIM), dtype=jnp.float32) * s_in, 'ws2': jax.random.normal(ks[6], (DIM, N_SHARED * INTER), dtype=jnp.float32) * s_hid, 'ws3': jax.random.normal(ks[7], (N_SHARED * INTER, DIM), dtype=jnp.float32) * s_in}
    _L0_ffn_in = _L0_ffn_setup()
    _d = {'L0_attn_x': _L0_attn_in['x'], 'L0_attn_Wq': _L0_attn_in['Wq'], 'L0_attn_Wkv': _L0_attn_in['Wkv'], 'L0_attn_q_scale': _L0_attn_in['q_scale'], 'L0_attn_k_scale': _L0_attn_in['k_scale'], 'L0_attn_Wg': _L0_attn_in['Wg'], 'L0_attn_bg': _L0_attn_in['bg'], 'L0_attn_Wo': _L0_attn_in['Wo'], 'L0_ffn_gate_w': _L0_ffn_in['gate_w'], 'L0_ffn_w1': _L0_ffn_in['w1'], 'L0_ffn_w2': _L0_ffn_in['w2'], 'L0_ffn_w3': _L0_ffn_in['w3'], 'L0_ffn_ws1': _L0_ffn_in['ws1'], 'L0_ffn_ws2': _L0_ffn_in['ws2'], 'L0_ffn_ws3': _L0_ffn_in['ws3']}
    _x0 = _d['L0_attn_x']
    _d['L0_attn_x'] = jax.random.normal(jax.random.fold_in(jax.random.key(seed), 1), (4, 1024, 512), dtype=_x0.dtype)
    del _x0
    return _d

def reference(L0_attn_x, L0_attn_Wq, L0_attn_Wkv, L0_attn_q_scale, L0_attn_k_scale, L0_attn_Wg, L0_attn_bg, L0_attn_Wo, L0_ffn_gate_w, L0_ffn_w1, L0_ffn_w2, L0_ffn_w3, L0_ffn_ws1, L0_ffn_ws2, L0_ffn_ws3):

    def _L0_attn_ref(x, Wq, Wkv, q_scale, k_scale, Wg, bg, Wo):
        import jax, jax.numpy as jnp
        import numpy as np
        B, N, D = (2, 1024, 512)
        H, DH, W = (8, 128, 128)
        SCALE = 8.0

        def _l2norm(t):
            return t / jnp.maximum(jnp.linalg.norm(t, axis=-1, keepdims=True), 1e-12)
        b, n, _ = x.shape
        inner = H * DH
        q = (x @ Wq.T).reshape(b, n, H, DH).transpose(0, 2, 1, 3)
        kv = x @ Wkv.T
        k = kv[..., :inner].reshape(b, n, H, DH).transpose(0, 2, 1, 3)
        v = kv[..., inner:].reshape(b, n, H, DH).transpose(0, 2, 1, 3)
        q = _l2norm(q) * q_scale
        k = _l2norm(k) * k_scale
        nb = n // W
        qb = q.reshape(b, H, nb, W, DH)
        kb = k.reshape(b, H, nb, W, DH)
        vb = v.reshape(b, H, nb, W, DH)

        def look_around(t):
            prev = jnp.concatenate([jnp.zeros_like(t[:, :, :1]), t[:, :, :-1]], axis=2)
            return jnp.concatenate([prev, t], axis=3)
        kw, vw = (look_around(kb), look_around(vb))
        pos = jnp.arange(n).reshape(nb, W)
        pos_prev = jnp.concatenate([jnp.full((1, W), -1), pos[:-1]], axis=0)
        posk = jnp.concatenate([pos_prev, pos], axis=1)
        dist = pos[:, :, None] - posk[:, None, :]
        mask = (posk[:, None, :] >= 0) & (dist >= 0) & (dist <= W)
        sim = jnp.einsum('bhnid,bhnjd->bhnij', qb * SCALE, kw)
        sim = jnp.where(mask, sim, jnp.finfo(sim.dtype).min)
        attn = jax.nn.softmax(sim, axis=-1)
        o = jnp.einsum('bhnij,bhnjd->bhnid', attn, vw).reshape(b, H, n, DH)
        gates = jax.nn.sigmoid(jnp.einsum('bnd,hd->bhn', x, Wg) + bg[None, :, None])
        o = o * gates[..., None]
        o = o.transpose(0, 2, 1, 3).reshape(b, n, inner)
        return o @ Wo.T

    def _L0_ffn_ref(x, gate_w, w1, w2, w3, ws1, ws2, ws3):
        import jax, jax.numpy as jnp
        import numpy as np
        B, S, DIM = (2, 512, 512)
        INTER = 256
        E = 8
        K = 2
        N_SHARED = 1
        ROUTE_SCALE = 1.0
        shape = x.shape
        xf = x.reshape(-1, DIM)
        scores = jax.nn.softmax(xf @ gate_w.T, axis=-1)
        weights, idx = jax.lax.top_k(scores, K)
        weights = weights * ROUTE_SCALE
        h = jnp.einsum('td,eid->eti', xf, w1)
        g = jax.nn.silu(h) * jnp.einsum('td,eid->eti', xf, w3)
        eo = jnp.einsum('eti,edi->etd', g, w2)
        comb = jnp.einsum('tke,tk->te', jax.nn.one_hot(idx, E, dtype=xf.dtype), weights)
        y = jnp.einsum('etd,te->td', eo, comb)
        z = jax.nn.silu(xf @ ws1.T) * (xf @ ws3.T) @ ws2.T
        return (y + z).reshape(shape)
    x = L0_attn_x
    x = _layernorm(x + _L0_attn_ref(x, L0_attn_Wq, L0_attn_Wkv, L0_attn_q_scale, L0_attn_k_scale, L0_attn_Wg, L0_attn_bg, L0_attn_Wo), axis=-1)
    x = _layernorm(x + _L0_ffn_ref(x, L0_ffn_gate_w, L0_ffn_w1, L0_ffn_w2, L0_ffn_w3, L0_ffn_ws1, L0_ffn_ws2, L0_ffn_ws3), axis=-1)
    return x

_drawn_inputs = setup_inputs


def setup_inputs(seed=0):
    import zlib

    import numpy as np

    out = dict(_drawn_inputs(seed))
    spreads = {'L0_attn_q_scale': (1.0, 0.6), 'L0_attn_k_scale': (1.0, 0.6), 'L0_attn_bg': (0.0, 0.8)}
    factors = {'L0_attn_Wq': 2.705, 'L0_attn_Wg': 5.837}
    for name, (base, spread) in spreads.items():
        noise = np.random.default_rng([zlib.crc32(name.encode()), seed]).standard_normal(out[name].shape)
        drawn = base * np.exp(spread * noise) if base else spread * noise
        out[name] = jnp.asarray(drawn.astype(out[name].dtype))
    for name, factor in factors.items():
        out[name] = (out[name] * factor).astype(out[name].dtype)
    return out
```

```python
from contextlib import ExitStack

import concourse.bass as bass
from concourse import mybir

ALU = mybir.AluOpType
ACT = mybir.ActivationFunctionType
F32 = mybir.dt.float32
F32R = mybir.dt.float32r
AX_X = mybir.AxisListType.X

P = 128
D = 512
DC = D // P
H = 8
T = 4096
NT = T // P
BLOCKS = 8
E = 8
U = E + 1
I = 256
IC = I // P
EPS = 1e-5
BIG = 1e38
GRP = 512
HPG = GRP // P
HALVES = 2
HT = NT // HALVES
GT = GRP // P
NG = HT // GT


def block_kernel(nc, x, xT, wqkvT, woT, wgT, bg, qs, ks, gateT, w13T, w2T, out):
    x2_d = nc.dram_tensor("x2_d", [T, D], F32, kind="Internal").ap()
    x2h_d = nc.dram_tensor("x2h_d", [P, DC, T], F32, kind="Internal").ap()
    x2l_d = nc.dram_tensor("x2l_d", [P, DC, T], F32, kind="Internal").ap()

    with ExitStack() as ctx:
        def sem(name):
            return ctx.enter_context(nc.semaphore(name))

        def sbuf(stack, name, shape, dt=F32):
            return stack.enter_context(nc.sbuf_tensor(name, shape, dt))

        bank = [ctx.enter_context(nc.psum_tensor(f"bank{i}", [P, GRP], F32)) for i in range(8)]
        psA, psS, psT, psO, psY = bank[0:2], bank[2:4], bank[4:6], bank[6], bank[7]

        ident = sbuf(ctx, "ident", [P, P])
        logits = sbuf(ctx, "logits", [P, NT, E])
        comb = sbuf(ctx, "comb", [P, NT, U])
        rstd = sbuf(ctx, "rstd", [P, 1])
        nhalf = sbuf(ctx, "nhalf", [P, HPG])
        bn6 = sbuf(ctx, "bn6", [P, 6])
        mv = sbuf(ctx, "mv", [P, 2])
        vareps = sbuf(ctx, "vareps", [P, 1])

        sa = ExitStack()
        wh = sbuf(sa, "wh", [P, DC, 3 * H * P], F32R)
        wl = sbuf(sa, "wl", [P, DC, 3 * H * P], F32R)
        woh = sbuf(sa, "woh", [P, H, D], F32R)
        wol = sbuf(sa, "wol", [P, H, D], F32R)
        wgs = sbuf(sa, "wgs", [P, 2, DC, E])
        wgh = sbuf(sa, "wgh", [P, 2, DC, E], F32R)
        wgl = sbuf(sa, "wgl", [P, 2, DC, E], F32R)
        bgb = sbuf(sa, "bgb", [P, H])
        qks = sbuf(sa, "qks", [P, 1])
        ksc = sbuf(sa, "ksc", [P, 1])
        prevm = sbuf(sa, "prevm", [P, P])
        flag = sbuf(sa, "flag", [P, NT // 2])
        mask = sbuf(sa, "mask", [P, 2, 2, P])
        xt = sbuf(sa, "xt", [P, 2, DC, P])
        xh = sbuf(sa, "xh", [P, 2, DC, P], F32R)
        xl = sbuf(sa, "xl", [P, 2, DC, P], F32R)
        xr = sbuf(sa, "xr", [P, 2, D])
        sq = sbuf(sa, "sq", [P, GRP])
        ssum = sbuf(sa, "ssum", [P, HPG])
        ssmax = sbuf(sa, "ssmax", [P, HPG])
        rnorm = sbuf(sa, "rnorm", [P, HPG])
        qkn = sbuf(sa, "qkn", [P, 4, GRP])
        qT = sbuf(sa, "qT", [P, H, P])
        kT = sbuf(sa, "kT", [P, 2, H, P])
        vv = sbuf(sa, "vv", [P, 2, H, P])
        pp = sbuf(sa, "pp", [P, H, 2 * P])
        mx = sbuf(sa, "mx", [P, H])
        nmx = sbuf(sa, "nmx", [P, H])
        esum = sbuf(sa, "esum", [P, H])
        zb = sbuf(sa, "zb", [P, H])
        ez = sbuf(sa, "ez", [P, H])
        gden = sbuf(sa, "gden", [P, H])
        gs = sbuf(sa, "gs", [P, H])
        pT = sbuf(sa, "pT", [P, HPG, 2 * P])
        oh = sbuf(sa, "oh", [P, H, P], F32R)
        ol = sbuf(sa, "ol", [P, H, P], F32R)
        x2h = sbuf(sa, "x2h", [P, DC, P], F32R)
        x2l = sbuf(sa, "x2l", [P, DC, P], F32R)
        r_a = pp[:, 0, 0:NT * E].rearrange("p (t e) -> p t e", e=E)
        r_b = pp[:, 1, 0:NT * E].rearrange("p (t e) -> p t e", e=E)
        r_c = pp[:, 2, 0:NT * E].rearrange("p (t e) -> p t e", e=E)
        r_d = pp[:, 3, 0:NT * E].rearrange("p (t e) -> p t e", e=E)
        r_e = pp[:, 4, 0:NT * E].rearrange("p (t e) -> p t e", e=E)
        r_m = sbuf(sa, "r_m", [P, NT])
        rev = sbuf(sa, "rev", [P, NT, E])
        stage = [qkn[:, :, :], pp[:, :, :].rearrange("p h (a c) -> p (h a c)", c=GRP // 2).rearrange("p (c n) -> p c n", n=GRP),
                 kT[:, :, :, :].rearrange("p s h d -> p (s h d)").rearrange("p (c n) -> p c n", n=GRP),
                 vv[:, :, :, :].rearrange("p s h d -> p (s h d)").rearrange("p (c n) -> p c n", n=GRP)]
        sa.close()

        sb = ExitStack()
        fh = sbuf(sb, "fh", [P, 2, DC + IC, GRP], F32R)
        fl = sbuf(sb, "fl", [P, 2, DC + IC, GRP], F32R)
        fs = sbuf(sb, "fs", [P, DC + IC, GRP])
        bh = sbuf(sb, "bh", [P, DC, HT * P], F32R)
        bl = sbuf(sb, "bl", [P, DC, HT * P], F32R)
        yy = sbuf(sb, "yy", [P, HT, D])
        sil = sbuf(sb, "sil", [P, IC, GRP])
        gg = sbuf(sb, "gg", [P, IC, GRP])
        gh = sbuf(sb, "gh", [P, 2, IC, GRP], F32R)
        gl = sbuf(sb, "gl", [P, 2, IC, GRP], F32R)
        oo = sbuf(sb, "oo", [P, 2, D])
        sb.close()

        small_in = sem("small_in")
        consts = sem("consts")
        kv_clear = sem("kv_clear")
        ident0 = sem("ident0")
        w_in = [sem(f"w_in{i}") for i in range(4)]
        w_hi = sem("w_hi")
        w_lo = sem("w_lo")
        wg_split = sem("wg_split")
        qks_s = sem("qks_s")
        xt_in = [sem(f"xt_in{i}") for i in range(2)]
        xr_in = [sem(f"xr_in{i}") for i in range(2)]
        x_hi = sem("x_hi")
        x_lo = sem("x_lo")
        proj = sem("proj")
        sq_s = sem("sq_s")
        ss_s = sem("ss_s")
        ssmax_s = sem("ssmax_s")
        rn_s = sem("rn_s")
        scaled = sem("scaled")
        z_read = sem("z_read")
        ez_s = sem("ez_s")
        v_s = sem("v_s")
        tr_s = sem("tr_s")
        trev = sem("trev")
        sim_s = sem("sim_s")
        mask_s = sem("mask_s")
        masked = sem("masked")
        nmx_s = sem("nmx_s")
        exp_s = sem("exp_s")
        gden_s = sem("gden_s")
        gs_s = sem("gs_s")
        pn_s = sem("pn_s")
        pt_s = sem("pt_s")
        ptev = sem("ptev")
        pv_s = sem("pv_s")
        o_hi = sem("o_hi")
        o_lo = sem("o_lo")
        wo_s = sem("wo_s")
        res_s = sem("res_s")
        bn_s = sem("bn_s")
        mv_s = sem("mv_s")
        ve_s = sem("ve_s")
        rstd_s = sem("rstd_s")
        x2_s = sem("x2_s")
        x2t_s = sem("x2t_s")
        x2_hi = sem("x2_hi")
        x2_lo = sem("x2_lo")
        lg_s = sem("lg_s")
        lg_read = sem("lg_read")
        x2_out = [sem(f"x2_out{i}") for i in range(2)]
        x2h_out = sem("x2h_out")
        x2l_out = sem("x2l_out")
        rt = sem("rt")
        rt_exp = sem("rt_exp")
        comb_s = sem("comb_s")
        f_in = sem("f_in")
        f_split = sem("f_split")
        b_in = sem("b_in")
        y_in = sem("y_in")
        h_s = sem("h_s")
        sil_s = sem("sil_s")
        gg_s = sem("gg_s")
        g_hi = sem("g_hi")
        g_lo = sem("g_lo")
        eo_s = sem("eo_s")
        y_s = sem("y_s")
        fbn = sem("fbn")
        fmv = sem("fmv")
        fve = sem("fve")
        frs = sem("frs")
        o_s = sem("o_s")
        o_out = [sem(f"o_out{i}") for i in range(2)]

        turns = {e.engine: sem(f"turns{n}") for n, e in enumerate((nc.sync, nc.gpsimd, nc.vector))}

        block = ctx.enter_context(nc.Block())

        QKV_COLS = [0, H * P, GRP, H * P + GRP, None, 2 * H * P, 2 * H * P + GRP]
        NW = 8

        def in_steps(eng, step):
            for s in range(4):
                step(s, s % 2)
            with eng.Fori(2, NT // 2) as i:
                step(2 * i, 0, middle=True)
                step(2 * i + 1, 1, middle=True)
            step(NT, 0)
            step(NT + 1, 1)

        def settled(eng):
            eng.sem_inc(turns[eng.engine], 1)

        def stages(s, middle):
            return (middle or s < NT), (middle or 1 <= s <= NT), (middle or s >= 2)

        @block.sync
        def _(sp):
            sp.dma_start(xt[:, 0, :, :], xT[:, 0:P].rearrange("(c p) n -> p c n", p=P)).then_inc(xt_in[0], 16)
            for n in range(NW):
                if n >= 4:
                    sp.wait_ge(w_lo, n - 3)
                if n < 6:
                    c0 = [0, H * P, GRP, H * P + GRP, 2 * H * P, 2 * H * P + GRP][n]
                    src = wqkvT[:, c0:c0 + GRP].rearrange("(c p) n -> p c n", p=P)
                else:
                    src = woT[(n - 6) * HPG * P:(n - 5) * HPG * P, :].rearrange("(c p) n -> p c n", p=P)
                sp.dma_start(stage[n % 4], src).then_inc(w_in[n % 4], 16)

            def step(s, par, middle=False):
                proj_on, attn_on, out_on = stages(s, middle)
                if middle or s + 1 < NT:
                    if middle or s >= 1:
                        sp.wait_ge(x_lo, s)
                        settled(sp)
                    sp.dma_start(xt[:, 1 - par, :, :],
                                 xT[:, bass.ds((s + 1) * P, P)].rearrange("(c p) n -> p c n", p=P))\
                      .then_inc(xt_in[1 - par], 16)
                if out_on:
                    w = s - 2
                    sp.wait_ge(x2_s, w + 1)
                    settled(sp)
                    sp.dma_start(x2_d[bass.ds(w * P, P), :], xr[:, par, :]).then_inc(x2_out[par], 16)
                if proj_on:
                    if middle or s >= 2:
                        sp.wait_ge(x2_out[par], 16 * (s // 2) if not middle else 8 * (s - par))
                        settled(sp)
                        sp.wait_ge(x2t_s, s - 1)
                        settled(sp)
                    sp.dma_start(xr[:, par, :], x[bass.ds(s * P, P), :]).then_inc(xr_in[par], 16)
                if out_on:
                    sp.wait_ge(x2_hi, w + 1)
                    settled(sp)
                    sp.dma_start(x2h_d[:, :, bass.ds(w * P, P)], x2h[:, :, :].bitcast(F32)).then_inc(x2h_out, 16)
                    sp.wait_ge(x2_lo, w + 1)
                    settled(sp)
                    sp.dma_start(x2l_d[:, :, bass.ds(w * P, P)], x2l[:, :, :].bitcast(F32)).then_inc(x2l_out, 16)

            in_steps(sp, step)

            for q in x2_out:
                sp.wait_ge(q, 16 * NT // 2)
            sp.wait_ge(x2h_out, 16 * NT)
            sp.wait_ge(x2l_out, 16 * NT)
            sp.wait_ge(comb_s, 1)

            def weights(h, e, n):
                if n is not None:
                    sp.wait_ge(f_split, 2 * n)
                    settled(sp)
                sp.dma_start(fs[:, 0:DC, :], w13T[bass.ds(e, 1), :, :].rearrange("a (c p) n -> p (a c) n", p=P))\
                  .then_inc(f_in, 16)
                sp.dma_start(fs[:, DC:DC + IC, :], w2T[bass.ds(e, 1), :, :].rearrange("a (c p) n -> p (a c) n", p=P))\
                  .then_inc(f_in, 16)

            for h in range(HALVES):
                weights(h, 0, U * h if h else None)
                if h:
                    sp.wait_ge(eo_s, HT * U * h)
                for part, dst in ((x2h_d, bh), (x2l_d, bl)):
                    sp.dma_start(dst[:, :, :].bitcast(F32), part[:, :, bass.ds(h * HT * P, HT * P)])\
                      .then_inc(b_in, 16)
                if h:
                    sp.wait_ge(o_s, HT * h)
                sp.dma_start(yy[:, :, :], x2_d[bass.ds(h * HT * P, HT * P), :].rearrange("(t p) n -> p t n", p=P))\
                  .then_inc(y_in, 16)
                with sp.Fori(1, U) as e:
                    weights(h, e, U * h + e)
                for t in range(HT):
                    sp.wait_ge(o_s, HT * h + t + 1)
                    settled(sp)
                    sp.dma_start(out[bass.ds(h * HT * P + t * P, P), :], oo[:, t % 2, :]).then_inc(o_out[t % 2], 16)
            for q in o_out:
                sp.wait_ge(q, 16 * NT // 2)

        @block.gpsimd
        def _(pool):
            pool.memset(ident[:, :], 0.0).then_inc(ident0, 1)
            pool.memset(nhalf[:, :], -0.5).then_inc(consts, 1)
            pool.memset(mask[:, :, :, :], 0.0).then_inc(ident0, 1)
            pool.memset(prevm[:, :], 0.0).then_inc(ident0, 1)
            pool.memset(flag[:, :], 0.0).then_inc(ident0, 1)
            pool.memset(comb[:, :, E:U], 1.0).then_inc(consts, 1)
            pool.iota(rev[:, :, :], pattern=[[0, NT], [-1, E]], base=E, channel_multiplier=0,
                      allow_small_or_imprecise_dtypes=True).then_inc(consts, 1)
            pool.wait_ge(ident0, 4)
            pool.affine_select(out=ident[:, :], in_=ident[:, :], compare_op=ALU.not_equal, fill=1.0, base=0,
                               pattern=[[-1, P]], channel_multiplier=1).then_inc(consts, 1)
            for slot in range(2):
                m = mask[:, slot, slot, :]
                pool.affine_select(out=m, in_=m, compare_op=ALU.is_ge, fill=-BIG, base=0,
                                   pattern=[[-1, P]], channel_multiplier=1).then_inc(consts, 1)
            for m in (mask[:, 1, 0, :], prevm[:, :]):
                pool.affine_select(out=m, in_=m, compare_op=ALU.is_ge, fill=-BIG, base=0,
                                   pattern=[[1, P]], channel_multiplier=-1).then_inc(consts, 1)
            for i in range(0, NT // 2, BLOCKS // 2):
                pool.memset(flag[:, i:i + 1], -BIG).then_inc(consts, 1)

            def split_x(s, par, first=False):
                pool.wait_ge(xt_in[par], 8 * (s - par) + 16)
                if not first:
                    pool.wait_ge(proj, 7 * (s - 1))
                settled(pool)
                pool.tensor_copy(xh[:, par, :, :], xt[:, par, :, :]).then_inc(x_hi, 1)
                pool.wait_ge(x_hi, s + 1)
                pool.tensor_tensor(xl[:, par, :, :], xt[:, par, :, :], xh[:, par, :, :].bitcast(F32), ALU.subtract)\
                    .then_inc(x_lo, 1)

            def power(n):
                pool.wait_ge(ssmax_s, n + 1)
                pool.wait_ge(scaled, n)
                pool.tensor_tensor(rnorm[:, :], ssmax[:, :], nhalf[:, :], ALU.pow).then_inc(rn_s, 1)

            def power0(n):
                pool.wait_ge(ssmax_s, n + 1)
                pool.tensor_tensor(rnorm[:, :], ssmax[:, :], nhalf[:, :], ALU.pow).then_inc(rn_s, 1)

            def normalise(u, g):
                pool.wait_ge(gs_s, 2 * u + g + 1)
                pool.wait_ge(exp_s, 2 * u + g + 1)
                pool.tensor_tensor(pp[:, g * HPG:(g + 1) * HPG, :], pp[:, g * HPG:(g + 1) * HPG, :],
                                   gs[:, g * HPG:(g + 1) * HPG].unsqueeze(2).to_broadcast([P, HPG, 2 * P]),
                                   ALU.mult).then_inc(pn_s, 1)

            def step(s, par, middle=False):
                proj_on, attn_on, out_on = stages(s, middle)
                if out_on:
                    pool.wait_ge(ve_s, s - 1)
                    pool.tensor_tensor(rstd[:, :], vareps[:, :], nhalf[:, 0:1], ALU.pow).then_inc(rstd_s, 1)
                if proj_on:
                    for j in range(3):
                        if j == 0 and not middle and s == 0:
                            power0(0)
                        else:
                            power(4 * s + j)
                if attn_on:
                    normalise(s - 1, 0)
                if proj_on:
                    power(4 * s + 3)
                if attn_on:
                    normalise(s - 1, 1)
                if middle or s + 1 < NT:
                    split_x(s + 1, 1 - par, first=(not middle and s == 0))

            split_x(0, 0, first=True)
            in_steps(pool, step)

            def split_w(h, e, slot, last_use):
                n = U * h + e
                pool.wait_ge(f_in, 32 * n + 32)
                if last_use is not None:
                    pool.wait_ge(eo_s, last_use)
                settled(pool)
                pool.tensor_copy(fh[:, slot, :, :], fs[:, :, :]).then_inc(f_split, 1)
                pool.wait_ge(f_split, 2 * n + 1)
                pool.tensor_tensor(fl[:, slot, :, :], fs[:, :, :], fh[:, slot, :, :].bitcast(F32), ALU.subtract)\
                    .then_inc(f_split, 1)

            for h in range(HALVES):
                split_w(h, 0, 0, HT * U * h if h else None)
                split_w(h, 1, 1, HT * U * h if h else None)
                with pool.Fori(1, U // 2) as i:
                    for k in range(2):
                        split_w(h, 2 * i + k, k, HT * (U * h + 2 * i + k - 1))
                split_w(h, U - 1, 0, HT * (U * h + U - 2))
                for t in range(HT):
                    pool.wait_ge(fve, HT * h + t + 1)
                    pool.tensor_tensor(rstd[:, :], vareps[:, :], nhalf[:, 0:1], ALU.pow).then_inc(frs, 1)

        @block.scalar
        def _(act):
            act.dma_start(wgs[:, 0, :, :], wgT.rearrange("(c p) n -> p c n", p=P)).then_inc(small_in, 16)
            act.dma_start(wgs[:, 1, :, :], gateT.rearrange("(c p) n -> p c n", p=P)).then_inc(small_in, 16)
            act.dma_start(bgb[:, :], bg.partition_broadcast(P)).then_inc(small_in, 16)
            act.dma_start(qks[:, :], qs.rearrange("(p a) -> p a", a=1)).then_inc(small_in, 16)
            act.dma_start(ksc[:, :], ks.rearrange("(p a) -> p a", a=1)).then_inc(small_in, 16)
            act.wait_ge(small_in, 80)
            act.activation(wgh[:, :, :, :], wgs[:, :, :, :], ACT.Copy).then_inc(wg_split, 1)
            for n in range(NW):
                act.wait_ge(w_in[n % 4], 16 * (n // 4 + 1))
                if n < 6:
                    c0 = [0, H * P, GRP, H * P + GRP, 2 * H * P, 2 * H * P + GRP][n]
                    dst = wh[:, :, c0:c0 + GRP]
                else:
                    dst = woh[:, (n - 6) * HPG:(n - 5) * HPG, :]
                act.activation(dst, stage[n % 4], ACT.Copy).then_inc(w_hi, 1)

            def squares(s, j, n, first=False):
                act.wait_ge(proj, 7 * s + j + 1)
                if not first:
                    act.wait_ge(ss_s, n)
                act.activation(sq[:, :], psA[j % 2][:, :], ACT.Square).then_inc(sq_s, 1)

            def heads_T(u, g, par, middle):
                act.wait_ge(tr_s, 4 * u + 2 * g + 1)
                if middle or u >= 1:
                    act.wait_ge(sim_s, 4 * (u - 1) + 2 * g + 2)
                act.activation(qT[:, g * HPG:(g + 1) * HPG, :], psT[0][:, :], ACT.Copy, scale=qks[:, 0:1])\
                   .then_inc(trev, 1)
                act.wait_ge(tr_s, 4 * u + 2 * g + 2)
                act.activation(kT[:, par, g * HPG:(g + 1) * HPG, :], psT[1][:, :], ACT.Copy).then_inc(trev, 1)

            def exps(u, g):
                act.wait_ge(nmx_s, 2 * u + g + 1)
                for h in range(g * HPG, (g + 1) * HPG):
                    ins = act.activation(pp[:, h, :], pp[:, h, :], ACT.Exp, bias=nmx[:, h:h + 1],
                                         accum_out=esum[:, h:h + 1])
                ins.then_inc(exp_s, 1)

            def p_T(u, g, first):
                for b in range(2):
                    act.wait_ge(pt_s, 4 * u + 2 * g + b + 1)
                    if b == 0 and not first:
                        act.wait_ge(pv_s, 2 * u + g)
                    act.activation(pT[:, 2 * b:2 * b + 2, :], psT[b][:, :], ACT.Copy).then_inc(ptev, 1)

            def o_high(u, g, first):
                act.wait_ge(pv_s, 2 * u + g + 1)
                if not first:
                    act.wait_ge(wo_s, u)
                act.activation(oh[:, g * HPG:(g + 1) * HPG, :], psO[:, :], ACT.Copy).then_inc(o_hi, 1)

            def v_copy(s, g, par, wait):
                act.wait_ge(proj, 7 * s + 6 + g)
                if wait:
                    act.wait_ge(pv_s, 2 * (s - 1) + g + 1)
                act.activation(vv[:, par, g * HPG:(g + 1) * HPG, :], psV[g], ACT.Copy)\
                   .then_inc(v_s, 1)

            psV = [psA[1][:, :], psA[0][:, :]]

            def step(s, par, middle=False):
                proj_on, attn_on, out_on = stages(s, middle)
                u, w = s - 1, s - 2
                first = not middle and s == 0
                u_first = not middle and s == 1
                if attn_on:
                    heads_T(u, 0, 1 - par, middle)
                if proj_on:
                    squares(s, 0, 4 * s, first=first)
                if attn_on:
                    heads_T(u, 1, 1 - par, middle)
                if proj_on:
                    squares(s, 1, 4 * s + 1)
                    squares(s, 2, 4 * s + 2)
                if attn_on:
                    exps(u, 0)
                if proj_on:
                    squares(s, 3, 4 * s + 3)
                if attn_on:
                    exps(u, 1)
                if attn_on:
                    p_T(u, 0, u_first)
                    o_high(u, 0, u_first)
                if proj_on:
                    v_copy(s, 0, par, attn_on)
                if attn_on:
                    p_T(u, 1, False)
                if out_on:
                    act.wait_ge(x2t_s, w + 1)
                    if middle or w >= 1:
                        act.wait_ge(x2h_out, 16 * w)
                        act.wait_ge(lg_s, w)
                    act.activation(x2h[:, :, :], psT[0][:, :], ACT.Copy).then_inc(x2_hi, 1)
                if attn_on:
                    o_high(u, 1, u_first)
                if proj_on:
                    v_copy(s, 1, par, attn_on)
                    act.wait_ge(z_read, s + 1)
                    if attn_on:
                        act.wait_ge(gden_s, 2 * s)
                    act.activation(ez[:, :], zb[:, :], ACT.Exp, scale=-1.0).then_inc(ez_s, 1)
                if out_on:
                    act.wait_ge(lg_s, w + 1)
                    act.activation(logits[:, bass.ds(w, 1), :], psY2(w), ACT.Copy).then_inc(lg_read, 1)

            def psY2(w):
                return psA[1][:, 0:E].unsqueeze(1)

            in_steps(act, step)
            act.wait_ge(rt, 2)
            act.activation(r_b, r_a, ACT.Exp).then_inc(rt_exp, 1)

            act.wait_ge(comb_s, 1)

            def group(n, g, gp, first=False):
                N = NG * n + g
                for m in range(IC):
                    act.wait_ge(h_s, 4 * N + 2 * m + 1)
                    if not first:
                        act.wait_ge(gg_s, 2 * (N - 1) + m + 1)
                    act.activation(sil[:, m, :], bank[2 * m][:, :], ACT.Silu).then_inc(sil_s, 1)
                for m in range(IC):
                    act.wait_ge(gg_s, 2 * N + m + 1)
                    if m == 0 and not (first or g == 1 and first is None):
                        act.wait_ge(eo_s, GT * (N - 1))
                    act.activation(gh[:, gp, m, :], gg[:, m, :], ACT.Copy).then_inc(g_hi, 1)

            group(0, 0, 0, first=True)
            for g in range(1, NG):
                group(0, g, g % 2)
            with act.Fori(1, HALVES * U) as n:
                for g in range(NG):
                    group(n, g, g % 2)

        @block.tensor
        def _(pe):
            pe.wait_ge(consts, 12)
            pe.wait_ge(wg_split, 2)

            def project(s, j, par, first, lg_before=False):
                b = psA[1] if j == 5 else psA[0] if j == 6 else psA[j % 2]
                if j == 0:
                    pe.wait_ge(x_lo, s + 1)
                    if not first:
                        pe.wait_ge(v_s, 2 * s)
                if j == 1 and not first:
                    pe.wait_ge(v_s, 2 * s)
                if j == 1 and lg_before:
                    pe.wait_ge(lg_read, s - 2)
                if j in (2, 3):
                    pe.wait_ge(scaled, 4 * s + j - 1)
                if j == 4:
                    pe.wait_ge(scaled, 4 * s + 3)
                if j == 5:
                    pe.wait_ge(scaled, 4 * s + 4)
                if j == 6:
                    pe.wait_ge(z_read, s + 1)
                if first and j != 4:
                    pe.wait_ge(w_lo, [1, 2, 3, 4, 0, 5, 6][j])
                for c in range(DC):
                    if j == 4:
                        prods = ((xh, wgh), (xh, wgl), (xl, wgh), (xl, wgl))
                        outp = b[:, 0:H]
                    else:
                        prods = ((xh, wh), (xh, wl), (xl, wh))
                        outp = b[:, :]
                    for k, (a, wt) in enumerate(prods):
                        rhs = wt[:, 0, c, :] if j == 4 else wt[:, c, QKV_COLS[j]:QKV_COLS[j] + GRP]
                        mm = pe.matmul(outp, a[:, par, c, :], rhs, start=(c == 0 and k == 0),
                                       stop=(c == DC - 1 and k == len(prods) - 1))
                mm.then_inc(proj, 1)

            def turn_qk(u, g, first):
                for b in range(2):
                    pe.wait_ge(scaled, 4 * u + 2 * g + b + 1)
                    if g == 1:
                        pe.wait_ge(trev, 4 * u + b + 1)
                    elif b == 0 and first is None:
                        pe.wait_ge(x2_lo, u - 1)
                        pe.wait_ge(ptev, 4 * u)
                    elif not first:
                        pe.wait_ge(ptev, 4 * u)
                    for h in range(HPG):
                        mm = pe.transpose(psT[b][:, h * P:(h + 1) * P], qkn[:, 2 * g + b, h * P:(h + 1) * P],
                                          ident[:, :])
                    mm.then_inc(tr_s, 1)

            def scores(u, g, first):
                pe.wait_ge(trev, 4 * u + 2 * g + 2)
                for b in range(2):
                    if not (first and g == 0):
                        pe.wait_ge(masked, 8 * u + 4 * (g - 1) + 2 * b + 2)
                    for hh in range(2):
                        h = g * HPG + 2 * b + hh
                        mm = pe.matmul(psS[b][:, hh * 2 * P:(hh + 1) * 2 * P], qT[:, h, :], kT[:, :, h, :],
                                       start=True, stop=True)
                    mm.then_inc(sim_s, 1)

            def turn_p(u, g):
                pe.wait_ge(pn_s, 2 * u + g + 1)
                for b in range(2):
                    if g == 0:
                        pe.wait_ge(trev, 4 * u + 3 + b)
                    else:
                        pe.wait_ge(ptev, 4 * u + 1 + b)
                    for hh in range(2):
                        for k in range(2):
                            mm = pe.transpose(psT[b][:, (2 * hh + k) * P:(2 * hh + k + 1) * P],
                                              pp[:, g * HPG + 2 * b + hh, k * P:(k + 1) * P], ident[:, :])
                    mm.then_inc(pt_s, 1)

            def values(u, g, first):
                pe.wait_ge(ptev, 4 * u + 2 * g + 2)
                pe.wait_ge(v_s, 2 * u + g + 1)
                if not (first and g == 0):
                    pe.wait_ge(o_lo, 2 * u + g)
                for hh in range(HPG):
                    for k in range(2):
                        mm = pe.matmul(psO[:, hh * P:(hh + 1) * P], vv[:, k, g * HPG + hh, :],
                                       pT[:, hh, k * P:(k + 1) * P], start=(k == 0), stop=(k == 1))
                mm.then_inc(pv_s, 1)

            def project_out(w, first):
                pe.wait_ge(o_lo, 2 * w + 2)
                if not first:
                    pe.wait_ge(res_s, w)
                else:
                    pe.wait_ge(w_lo, NW)
                for h in range(H):
                    for k, (a, b) in enumerate(((oh, woh), (oh, wol), (ol, woh))):
                        mm = pe.matmul(psY[:, :], a[:, h, :], b[:, h, :], start=(h == 0 and k == 0),
                                       stop=(h == H - 1 and k == 2))
                mm.then_inc(wo_s, 1)

            def turn_x2(w, par):
                pe.wait_ge(x2_s, w + 1)
                for c in range(DC):
                    mm = pe.transpose(psT[0][:, c * P:(c + 1) * P], xr[:, par, c * P:(c + 1) * P], ident[:, :])
                mm.then_inc(x2t_s, 1)

            def router(w):
                pe.wait_ge(x2_lo, w + 1)
                for c in range(DC):
                    for k, (a, b) in enumerate(((x2h, wgh), (x2h, wgl), (x2l, wgh), (x2l, wgl))):
                        mm = pe.matmul(psA[1][:, 0:E], a[:, c, :], b[:, 1, c, :], start=(c == 0 and k == 0),
                                       stop=(c == DC - 1 and k == 3))
                mm.then_inc(lg_s, 1)

            def step(s, par, middle=False):
                proj_on, attn_on, out_on = stages(s, middle)
                u, w = s - 1, s - 2
                first = not middle and s == 0
                u_first = not middle and s == 1
                w_first = not middle and s == 2
                lg_before = middle or s >= 3
                if attn_on:
                    turn_qk(u, 0, None if (middle or s >= 3) else u_first)
                if out_on:
                    project_out(w, w_first)
                if proj_on:
                    project(s, 0, par, first)
                if attn_on:
                    turn_qk(u, 1, u_first)
                if proj_on:
                    project(s, 1, par, first, lg_before)
                if attn_on:
                    scores(u, 0, u_first)
                if proj_on:
                    project(s, 2, par, first)
                if attn_on:
                    scores(u, 1, u_first)
                if proj_on:
                    project(s, 3, par, first)
                    project(s, 4, par, first)
                if attn_on:
                    turn_p(u, 0)
                if proj_on:
                    project(s, 5, par, first)
                if attn_on:
                    values(u, 0, u_first)
                    turn_p(u, 1)
                if proj_on:
                    project(s, 6, par, first)
                if attn_on:
                    values(u, 1, u_first)
                if out_on:
                    if attn_on:
                        pe.wait_ge(ptev, 4 * u + 4)
                    turn_x2(w, par)
                    if proj_on:
                        pe.wait_ge(v_s, 2 * s + 1)
                    router(w)

            in_steps(pe, step)

            pe.wait_ge(comb_s, 1)
            pe.wait_ge(b_in, 32)

            def hidden(n, g, slot, first=False):
                N = NG * n + g
                if g == 0:
                    pe.wait_ge(f_split, 2 * n + 2)
                for m in range(IC):
                    for k in range(2):
                        if not first:
                            if k == 0:
                                pe.wait_ge(sil_s, 2 * (N - 1) + m + 1)
                            else:
                                pe.wait_ge(gg_s, 2 * (N - 1) + m + 1)
                        cols = k * I + m * P
                        q = 0
                        for c in range(DC):
                            for a, b in ((fh, bh), (fh, bl), (fl, bh)):
                                mm = pe.matmul(bank[2 * m + k][:, :], a[:, slot, c, cols:cols + P],
                                               b[:, c, g * GRP:(g + 1) * GRP], start=(q == 0), stop=(q == 3 * DC - 1))
                                q += 1
                        mm.then_inc(h_s, 1)

            def expert_out(n, g, slot, gp, first=False):
                N = NG * n + g
                pe.wait_ge(g_lo, 2 * N + 2)
                for t in range(GT):
                    if not first:
                        pe.wait_ge(y_s, GT * (N - 1) + t + 1)
                    q = 0
                    for m in range(IC):
                        for a, b in ((gh, fh), (gh, fl), (gl, fh)):
                            mm = pe.matmul(bank[4 + t][:, :], a[:, gp, m, t * P:(t + 1) * P], b[:, slot, DC + m, :],
                                           start=(q == 0), stop=(q == 3 * IC - 1))
                            q += 1
                    mm.then_inc(eo_s, 1)

            def unit(n, slot, before, first=False):
                for g in range(NG):
                    hidden(n, g, slot, first=first and g == 0)
                    if g == 0:
                        if before:
                            expert_out(n - 1, NG - 1, 1 - slot, (NG - 1) % 2)
                    else:
                        expert_out(n, g - 1, slot, (g - 1) % 2, first=first and g == 1)

            def half(n0, first):
                unit(n0, 0, False, first=first)
                with pe.Fori(0, (U - 1) // 2) as i:
                    unit(n0 + 2 * i + 1, 1, True)
                    unit(n0 + 2 * i + 2, 0, True)
                expert_out(n0 + U - 1, NG - 1, 0, (NG - 1) % 2)

            half(0, True)
            pe.wait_ge(b_in, 64)
            half(U, False)

        @block.vector
        def _(dve):
            dve.wait_ge(small_in, 80)
            dve.wait_ge(wg_split, 1)
            dve.tensor_tensor(wgl[:, :, :, :], wgs[:, :, :, :], wgh[:, :, :, :].bitcast(F32), ALU.subtract)\
               .then_inc(wg_split, 1)
            dve.scalar_tensor_tensor(out=qks[:, :], in0=qks[:, :], scalar=8.0, in1=ksc[:, :],
                                     op0=ALU.mult, op1=ALU.mult).then_inc(qks_s, 1)
            for n in range(NW):
                dve.wait_ge(w_hi, n + 1)
                if n < 6:
                    c0 = [0, H * P, GRP, H * P + GRP, 2 * H * P, 2 * H * P + GRP][n]
                    hi, lo = wh[:, :, c0:c0 + GRP], wl[:, :, c0:c0 + GRP]
                else:
                    hi, lo = (q[:, (n - 6) * HPG:(n - 5) * HPG, :] for q in (woh, wol))
                dve.tensor_tensor(lo, stage[n % 4], hi.bitcast(F32), ALU.subtract).then_inc(w_lo, 1)
            dve.wait_ge(w_lo, NW)
            dve.memset(kT[:, 1, :, :], 0.0).then_inc(kv_clear, 1)
            dve.memset(vv[:, 1, :, :], 0.0).then_inc(kv_clear, 1)
            dve.wait_ge(kv_clear, 2)
            dve.wait_ge(consts, 12)

            def sums(s, j, first=False):
                n = 4 * s + j
                dve.wait_ge(sq_s, n + 1)
                if not first:
                    dve.wait_ge(ssmax_s, n)
                dve.tensor_reduce(ssum[:, :], sq[:, :].rearrange("p (h d) -> p h d", d=P), AX_X, ALU.add)\
                   .then_inc(ss_s, 1)
                dve.wait_ge(ss_s, n + 1)
                if not first:
                    dve.wait_ge(rn_s, n)
                dve.tensor_scalar(ssmax[:, :], ssum[:, :], 1e-24, None, ALU.max).then_inc(ssmax_s, 1)

            def scale(s, j, attn_on):
                n = 4 * s + j
                dve.wait_ge(rn_s, n + 1)
                if attn_on:
                    dve.wait_ge(tr_s, 4 * (s - 1) + j + 1)
                dve.tensor_tensor(qkn[:, j, :].rearrange("p (h d) -> p h d", d=P),
                                  psA[j % 2][:, :].rearrange("p (h d) -> p h d", d=P),
                                  rnorm[:, :].unsqueeze(2).to_broadcast([P, HPG, P]), ALU.mult).then_inc(scaled, 1)

            def mask_max(u, g, upar, first):
                for b in range(2):
                    dve.wait_ge(sim_s, 4 * u + 2 * g + b + 1)
                    if b == 0 and not first:
                        dve.wait_ge(pt_s, 4 * (u - 1) + 2 * g + 2)
                        dve.wait_ge(exp_s, 2 * (u - 1) + g + 1)
                    settled(dve)
                    for hh in range(2):
                        h = g * HPG + 2 * b + hh
                        dve.tensor_tensor_reduce(
                            pp[:, h, :], psS[b][:, hh * 2 * P:(hh + 1) * 2 * P],
                            mask[:, upar, :, :].rearrange("p k j -> p (k j)"), 1.0, -3e38, ALU.add, ALU.max,
                            mx[:, h:h + 1]).then_inc(masked, 1)
                dve.wait_ge(masked, 8 * u + 4 * g + 4)
                dve.tensor_scalar(nmx[:, g * HPG:(g + 1) * HPG], mx[:, g * HPG:(g + 1) * HPG], -1.0, None, ALU.mult)\
                   .then_inc(nmx_s, 1)

            def gate_scale(u, g, first):
                c = slice(g * HPG, (g + 1) * HPG)
                dve.wait_ge(exp_s, 2 * u + g + 1)
                if g == 0:
                    dve.wait_ge(ez_s, u + 1)
                dve.scalar_tensor_tensor(out=gden[:, c], in0=ez[:, c], scalar=1.0, in1=esum[:, c],
                                         op0=ALU.add, op1=ALU.mult).then_inc(gden_s, 1)
                dve.wait_ge(gden_s, 2 * u + g + 1)
                if not first:
                    dve.wait_ge(pn_s, 2 * (u - 1) + g + 1)
                dve.reciprocal(gs[:, c], gden[:, c]).then_inc(gs_s, 1)

            def o_low(u, g):
                dve.wait_ge(o_hi, 2 * u + g + 1)
                dve.tensor_tensor(ol[:, g * HPG:(g + 1) * HPG, :].rearrange("p h d -> p (h d)"), psO[:, :],
                                  oh[:, g * HPG:(g + 1) * HPG, :].rearrange("p h d -> p (h d)").bitcast(F32),
                                  ALU.subtract).then_inc(o_lo, 1)

            def layernorm_stats(src, n, bn, m, v, prev):
                dve.bn_stats(bn6[:, :], src).then_inc(bn, 1)
                dve.wait_ge(bn, n + 1)
                settled(dve)
                dve.bn_aggr(mv[:, :], bn6[:, :]).then_inc(m, 1)
                dve.wait_ge(m, n + 1)
                if prev:
                    dve.wait_ge(prev, n)
                dve.tensor_scalar(vareps[:, :], mv[:, 1:2], EPS, None, ALU.add).then_inc(v, 1)

            def step(s, par, middle=False):
                proj_on, attn_on, out_on = stages(s, middle)
                u, w = s - 1, s - 2
                first = not middle and s == 0
                u_first = not middle and s == 1
                w_first = not middle and s == 2
                if out_on:
                    dve.wait_ge(wo_s, w + 1)
                    dve.wait_ge(xr_in[par], 8 * (w - par) + 16)
                    dve.tensor_tensor(xr[:, par, :], psY[:, :], xr[:, par, :], ALU.add).then_inc(res_s, 1)
                    dve.wait_ge(res_s, w + 1)
                    layernorm_stats(xr[:, par, :], w, bn_s, mv_s, ve_s, None if w_first else rstd_s)
                if proj_on:
                    sums(s, 0, first)
                if out_on:
                    dve.wait_ge(rstd_s, w + 1)
                    dve.tensor_scalar(xr[:, par, :], xr[:, par, :], mv[:, 0:1], rstd[:, 0:1], ALU.subtract, ALU.mult)\
                       .then_inc(x2_s, 1)
                if proj_on:
                    scale(s, 0, attn_on)
                    sums(s, 1)
                if attn_on:
                    mask_max(u, 0, 1 - par, u_first)
                if proj_on:
                    scale(s, 1, attn_on)
                    sums(s, 2)
                if attn_on:
                    mask_max(u, 1, 1 - par, u_first)
                if attn_on:
                    gate_scale(u, 0, u_first)
                if proj_on:
                    scale(s, 2, attn_on)
                    sums(s, 3)
                if attn_on:
                    gate_scale(u, 1, u_first)
                if proj_on:
                    scale(s, 3, attn_on)
                    dve.wait_ge(proj, 7 * s + 5)
                    if not first:
                        dve.wait_ge(ez_s, s)
                    dve.tensor_tensor(zb[:, :], psA[0][:, 0:H], bgb[:, :], ALU.add).then_inc(z_read, 1)
                if attn_on:
                    o_low(u, 0)
                if out_on:
                    dve.wait_ge(x2_hi, w + 1)
                    if not w_first:
                        dve.wait_ge(x2l_out, 16 * w)
                    dve.tensor_tensor(x2l[:, :, :].rearrange("p c n -> p (c n)"), psT[0][:, :],
                                      x2h[:, :, :].rearrange("p c n -> p (c n)").bitcast(F32), ALU.subtract)\
                       .then_inc(x2_lo, 1)
                if attn_on:
                    o_low(u, 1)

            in_steps_dve(dve, step, mask, prevm, flag, masked, mask_s)

            def chained(ins):
                route_step[0] += 1
                ins.then_inc(rt, 1)
                dve.wait_ge(rt, route_step[0])

            route_step = [0]
            wide = [P, NT, E]
            dve.wait_ge(lg_read, NT)
            dve.wait_ge(pt_s, 4 * NT)
            chained(dve.tensor_reduce(r_m[:, :], logits[:, :, :], AX_X, ALU.max))
            chained(dve.tensor_tensor(r_a, logits[:, :, :], r_m[:, :].unsqueeze(2).to_broadcast(wide), ALU.subtract))
            dve.wait_ge(rt_exp, 1)
            chained(dve.tensor_reduce(r_m[:, :], r_b, AX_X, ALU.add))
            chained(dve.reciprocal(r_m[:, :], r_m[:, :]))
            chained(dve.tensor_tensor(r_b, r_b, r_m[:, :].unsqueeze(2).to_broadcast(wide), ALU.mult))
            chained(dve.tensor_copy(r_c, r_b))
            for k in range(2):
                chained(dve.tensor_reduce(r_m[:, :], r_c, AX_X, ALU.max))
                chained(dve.tensor_tensor(r_a, r_c, r_m[:, :].unsqueeze(2).to_broadcast(wide), ALU.is_equal))
                chained(dve.tensor_tensor(r_a, r_a, rev[:, :, :], ALU.mult))
                chained(dve.tensor_reduce(r_m[:, :], r_a, AX_X, ALU.max))
                chained(dve.tensor_tensor([r_d, r_e][k], rev[:, :, :], r_m[:, :].unsqueeze(2).to_broadcast(wide),
                                          ALU.is_equal))
                if k == 0:
                    chained(dve.scalar_tensor_tensor(out=r_c, in0=r_d, scalar=-2.0, in1=r_b, op0=ALU.mult,
                                                     op1=ALU.add))
            chained(dve.tensor_tensor(r_d, r_d, r_e, ALU.add))
            dve.tensor_tensor(comb[:, :, 0:E], r_b, r_d, ALU.mult).then_inc(comb_s, 1)
            dve.wait_ge(comb_s, 1)

            def products(n, g, gp, first=False):
                N = NG * n + g
                for m in range(IC):
                    dve.wait_ge(h_s, 4 * N + 2 * m + 2)
                    dve.wait_ge(sil_s, 2 * N + m + 1)
                    if not first:
                        dve.wait_ge(g_lo, 2 * (N - 1) + m + 1)
                    dve.tensor_tensor(gg[:, m, :], bank[2 * m + 1][:, :], sil[:, m, :], ALU.mult).then_inc(gg_s, 1)
                for m in range(IC):
                    dve.wait_ge(g_hi, 2 * N + m + 1)
                    dve.tensor_tensor(gl[:, gp, m, :], gg[:, m, :], gh[:, gp, m, :].bitcast(F32), ALU.subtract)\
                       .then_inc(g_lo, 1)

            def add_out(h, n, e, g):
                N = NG * n + g
                for t in range(GT):
                    dve.wait_ge(eo_s, GT * N + t + 1)
                    tile = GT * g + t
                    dve.scalar_tensor_tensor(out=yy[:, tile, :], in0=bank[4 + t][:, :],
                                             scalar=comb_at(h, tile, e), in1=yy[:, tile, :],
                                             op0=ALU.mult, op1=ALU.add).then_inc(y_s, 1)

            comb_flat = comb[:, :, :].rearrange("p t e -> p (t e)")

            def comb_at(h, tile, e):
                return comb_flat[:, bass.ds((h * HT + tile) * U + e, 1)]

            def last_norm(h, n, t):
                q = HT * h + t
                dve.wait_ge(y_s, NG * GT * n + t + 1)
                dve.bn_stats(bn6[:, :], yy[:, t, :]).then_inc(fbn, 1)
                dve.wait_ge(fbn, q + 1)
                settled(dve)
                dve.bn_aggr(mv[:, :], bn6[:, :]).then_inc(fmv, 1)
                dve.wait_ge(fmv, q + 1)
                dve.tensor_scalar(vareps[:, :], mv[:, 1:2], EPS, None, ALU.add).then_inc(fve, 1)
                dve.wait_ge(frs, q + 1)
                if h > 0 or t >= 2:
                    dve.wait_ge(o_out[t % 2], 16 * (HT * h // 2 + t // 2))
                dve.tensor_scalar(oo[:, t % 2, :], yy[:, t, :], mv[:, 0:1], rstd[:, 0:1], ALU.subtract, ALU.mult)\
                   .then_inc(o_s, 1)

            def unit(h, n, e, before, last=False, first=False):
                for g in range(NG):
                    products(n, g, g % 2, first=first and g == 0)
                    if g == 0:
                        if before:
                            add_out(h, n - 1, e - 1, NG - 1)
                    else:
                        add_out(h, n, e, g - 1)

            for h in range(HALVES):
                n0 = U * h
                dve.wait_ge(y_in, 16 * (h + 1))
                unit(h, n0, 0, False, first=(h == 0))
                with dve.Fori(0, (U - 1) // 2) as i:
                    unit(h, n0 + 2 * i + 1, 2 * i + 1, True)
                    unit(h, n0 + 2 * i + 2, 2 * i + 2, True)
                add_out(h, n0 + U - 1, U - 1, NG - 1)
                for t in range(HT):
                    last_norm(h, n0 + U - 1, t)


def in_steps_dve(dve, step, mask, prevm, flag, masked, mask_s):
    def set_mask(s, i, first=False):
        if not first:
            dve.wait_ge(masked, 8 * (s - 1))
        dve.tensor_scalar(mask[:, 0, 1, :], prevm[:, :], flag[:, bass.ds(i, 1)], None, ALU.add).then_inc(mask_s, 1)
        dve.wait_ge(mask_s, i + 1)

    for s in range(4):
        if s % 2:
            set_mask(s, s // 2, first=(s == 1))
        step(s, s % 2)
    with dve.Fori(2, NT // 2) as i:
        step(2 * i, 0, middle=True)
        set_mask(2 * i + 1, i)
        step(2 * i + 1, 1, middle=True)
    step(NT, 0)
    step(NT + 1, 1)


_INS = ["x", "xT", "wqkvT", "woT", "wgT", "bg", "qs", "ks", "gateT", "w13T", "w2T"]


def kernel(**inputs):
    import numpy as _np
    import concourse.bacc as _bacc
    from concourse import mybir as _mybir
    from concourse.bass_utils import run_bass_kernel_spmd as _run

    a = {k: _np.asarray(v) for k, v in inputs.items()}
    x = a["L0_attn_x"].reshape(T, D)
    w13 = _np.concatenate([_np.concatenate([a["L0_ffn_w1"], a["L0_ffn_w3"]], axis=1),
                           _np.concatenate([a["L0_ffn_ws1"], a["L0_ffn_ws3"]], axis=0)[None]], axis=0)
    w2 = _np.concatenate([a["L0_ffn_w2"], a["L0_ffn_ws2"][None]], axis=0)
    laid = {
        "x": x,
        "xT": _np.pad(x.T, ((0, 0), (0, P))),
        "wqkvT": _np.concatenate([a["L0_attn_Wq"], a["L0_attn_Wkv"]], axis=0).T,
        "woT": a["L0_attn_Wo"].T,
        "wgT": a["L0_attn_Wg"].T,
        "bg": a["L0_attn_bg"],
        "qs": a["L0_attn_q_scale"],
        "ks": a["L0_attn_k_scale"],
        "gateT": a["L0_ffn_gate_w"].T,
        "w13T": w13.transpose(0, 2, 1),
        "w2T": w2.transpose(0, 2, 1),
    }
    nc = _bacc.Bacc("TRN2", target_bir_lowering=False, num_devices=1)
    arrays, args = {}, []
    for name in _INS:
        arr = _np.ascontiguousarray(laid[name])
        arrays[f"in_{name}"] = arr
        args.append(nc.dram_tensor(f"in_{name}", arr.shape, _mybir.dt.from_np(arr.dtype), kind="ExternalInput").ap())
    out = nc.dram_tensor("out_0", (T, D), F32, kind="ExternalOutput").ap()
    block_kernel(nc, *args, out)
    r = _run(nc, [arrays], core_ids=[0])
    return r.results[0]["out_0"].reshape(a["L0_attn_x"].shape)
```

```python
from contextlib import ExitStack

import concourse.bass as bass
from concourse import mybir

ALU = mybir.AluOpType
ACT = mybir.ActivationFunctionType
F32 = mybir.dt.float32
F32R = mybir.dt.float32r
U32 = mybir.dt.uint32
I32 = mybir.dt.int32
AX_X = mybir.AxisListType.X

P = 128
D = 512
DC = D // P
H = 8
T = 4096
NT = T // P
BLOCKS = 8
E = 8
U = E + 1
I = 256
IC = I // P
EPS = 1e-5
BIG = 1e38
GRP = 512
HPG = GRP // P
NX = (2 * T + E * (P - 1)) // P
NX += NX % 2
S1 = 20
NQ = NX + NT
NSC = 2 * NT


def block_kernel(nc, x, xT, wqkvT, woT, wgT, bg, qs, ks, gateT, w13T, w2T, out):
    x2_d = nc.dram_tensor("x2_d", [T, D], F32, kind="Internal").ap()
    tok_d = nc.dram_tensor("tok_d", [NX * P, 1], F32, kind="Internal").ap()
    eo_d = nc.dram_tensor("eo_d", [NX * P, D], F32, kind="Internal").ap()
    z_d = nc.dram_tensor("z_d", [T, D], F32, kind="Internal").ap()

    with ExitStack() as ctx:
        def sem(name):
            return ctx.enter_context(nc.semaphore(name))

        def sbuf(stack, name, shape, dt=F32):
            return stack.enter_context(nc.sbuf_tensor(name, shape, dt))

        bank = [ctx.enter_context(nc.psum_tensor(f"bank{i}", [P, GRP], F32)) for i in range(8)]
        psA, psS, psT, psO, psY = bank[0:2], bank[2:4], bank[4:6], bank[6], bank[7]

        ident = sbuf(ctx, "ident", [P, P])
        logits = sbuf(ctx, "logits", [P, NT, 2 * E])
        rstd = sbuf(ctx, "rstd", [P, 1])
        nhalf = sbuf(ctx, "nhalf", [P, HPG])
        bn6 = sbuf(ctx, "bn6", [P, 6])
        mv = sbuf(ctx, "mv", [P, 2])
        vareps = sbuf(ctx, "vareps", [P, 1])
        tok = sbuf(ctx, "tok", [P, NT])
        slot_u = sbuf(ctx, "slot_u", [P, 2, NT], U32)
        wt2 = sbuf(ctx, "wt2", [P, 2, NT])
        idx_u = sbuf(ctx, "idx_u", [P, NX], U32)
        zt = sbuf(ctx, "zt", [P, NX])
        expert_of = sbuf(ctx, "expert_of", [P, NX], I32)

        sa = ExitStack()
        wh = sbuf(sa, "wh", [P, DC, 3 * H * P], F32R)
        wl = sbuf(sa, "wl", [P, DC, 3 * H * P], F32R)
        woh = sbuf(sa, "woh", [P, H, D], F32R)
        wol = sbuf(sa, "wol", [P, H, D], F32R)
        wgs = sbuf(sa, "wgs", [P, 2, DC, E])
        wgp = sbuf(sa, "wgp", [P, 2, DC, 2, E], F32R)
        bgb = sbuf(sa, "bgb", [P, H])
        qks = sbuf(sa, "qks", [P, 1])
        ksc = sbuf(sa, "ksc", [P, 1])
        prevm = sbuf(sa, "prevm", [P, P])
        flag = sbuf(sa, "flag", [P, NT // 2])
        mask = sbuf(sa, "mask", [P, 2, 2, P])
        xt = sbuf(sa, "xt", [P, 2, DC, P])
        xh = sbuf(sa, "xh", [P, 2, DC, P], F32R)
        xl = sbuf(sa, "xl", [P, 2, DC, P], F32R)
        xr = sbuf(sa, "xr", [P, 2, D])
        sq = sbuf(sa, "sq", [P, GRP])
        ssum = sbuf(sa, "ssum", [P, HPG])
        ssmax = sbuf(sa, "ssmax", [P, HPG])
        rnorm = sbuf(sa, "rnorm", [P, HPG])
        qkn = sbuf(sa, "qkn", [P, 4, GRP])
        qT = sbuf(sa, "qT", [P, H, P])
        kT = sbuf(sa, "kT", [P, 2, H, P])
        vv = sbuf(sa, "vv", [P, 2, H, P])
        pp = sbuf(sa, "pp", [P, H, 2 * P])
        mx = sbuf(sa, "mx", [P, H])
        nmx = sbuf(sa, "nmx", [P, H])
        esum = sbuf(sa, "esum", [P, H])
        zt8 = sbuf(sa, "zt8", [P, H])
        zb = sbuf(sa, "zb", [P, H])
        ez = sbuf(sa, "ez", [P, H])
        gden = sbuf(sa, "gden", [P, H])
        gs = sbuf(sa, "gs", [P, H])
        pT = sbuf(sa, "pT", [P, HPG, 2 * P])
        oh = sbuf(sa, "oh", [P, H, P], F32R)
        ol = sbuf(sa, "ol", [P, H, P], F32R)
        x2h = sbuf(sa, "x2h", [P, DC, P], F32R)
        x2l = sbuf(sa, "x2l", [P, DC, P], F32R)
        stage = [qkn[:, :, :], pp[:, :, :].rearrange("p h (a c) -> p (h a c)", c=GRP // 2).rearrange("p (c n) -> p c n", n=GRP),
                 kT[:, :, :, :].rearrange("p s h d -> p (s h d)").rearrange("p (c n) -> p c n", n=GRP),
                 vv[:, :, :, :].rearrange("p s h d -> p (s h d)").rearrange("p (c n) -> p c n", n=GRP)]
        sa.close()

        sb = ExitStack()
        w13h = sbuf(sb, "w13h", [P, E, DC, GRP], F32R)
        w13l = sbuf(sb, "w13l", [P, E, DC, GRP], F32R)
        sh13h = sbuf(sb, "sh13h", [P, DC, GRP], F32R)
        sh13l = sbuf(sb, "sh13l", [P, DC, GRP], F32R)
        sh2 = sbuf(sb, "sh2", [P, IC, GRP])
        bx = sbuf(sb, "bx", [P, 2, D])
        bh = sbuf(sb, "bh", [P, 2, DC, P], F32R)
        bl = sbuf(sb, "bl", [P, 2, DC, P], F32R)
        sil = sbuf(sb, "sil", [P, 2, I])
        gg = sbuf(sb, "gg", [P, 2, I])
        gT = sbuf(sb, "gT", [P, 2, IC, P])
        eo = sbuf(sb, "eo", [P, 2, D])
        idxc = sbuf(sb, "idxc", [P, 2, 1], U32)
        s1 = ExitStack()
        fs = sbuf(s1, "fs", [P, DC, GRP])
        wide_t = [sbuf(s1, f"r{n}", [P, NT, E]) for n in range(7)]
        r_m = sbuf(s1, "r_m", [P, NT])
        rev = sbuf(s1, "rev", [P, NT, E])
        tri = sbuf(s1, "tri", [P, P])
        ones = sbuf(s1, "ones", [P, P])
        carry = sbuf(s1, "carry", [P, E, NT])
        tot = sbuf(s1, "tot", [P, E, NT])
        inc = sbuf(s1, "inc", [P, E, NT])
        small = sbuf(s1, "small", [P, 6, E])
        small_i = sbuf(s1, "small_i", [P, 2, E], I32)
        jx = sbuf(s1, "jx", [P, NX, E])
        tok_t = sbuf(s1, "tok_t", [NX, P])
        s1.close()
        s2 = ExitStack()
        w2e = sbuf(s2, "w2e", [P, E, IC, GRP])
        s2.close()
        s3 = ExitStack()
        ga = sbuf(s3, "ga", [P, 2, 2, D])
        gb = sbuf(s3, "gb", [P, 2, 2, D])
        zl = sbuf(s3, "zl", [P, 2, 2, D])
        xres = sbuf(s3, "xres", [P, 2, D])
        oo = sbuf(s3, "oo", [P, 2, D])
        ic = sbuf(s3, "ic", [P, 2, 4], U32)
        ve2 = sbuf(s3, "ve2", [P, 2])
        mv2 = sbuf(s3, "mv2", [P, 2, 2, 2])
        rs2 = sbuf(s3, "rs2", [P, 2, 2])
        s3.close()
        sb.close()

        small_in = sem("small_in")
        consts = sem("consts")
        kv_clear = sem("kv_clear")
        ident0 = sem("ident0")
        w_in = [sem(f"w_in{i}") for i in range(4)]
        w_hi = sem("w_hi")
        w_lo = sem("w_lo")
        wg_split = sem("wg_split")
        qks_s = sem("qks_s")
        xt_in = [sem(f"xt_in{i}") for i in range(2)]
        xr_in = [sem(f"xr_in{i}") for i in range(2)]
        x_hi = sem("x_hi")
        x_lo = sem("x_lo")
        proj = sem("proj")
        sq_s = sem("sq_s")
        ss_s = sem("ss_s")
        ssmax_s = sem("ssmax_s")
        rn_s = sem("rn_s")
        scaled = sem("scaled")
        z_half = sem("z_half")
        z_read = sem("z_read")
        ez_s = sem("ez_s")
        v_s = sem("v_s")
        tr_s = sem("tr_s")
        trev = sem("trev")
        sim_s = sem("sim_s")
        mask_s = sem("mask_s")
        masked = sem("masked")
        nmx_s = sem("nmx_s")
        exp_s = sem("exp_s")
        gden_s = sem("gden_s")
        gs_s = sem("gs_s")
        pn_s = sem("pn_s")
        pt_s = sem("pt_s")
        ptev = sem("ptev")
        pv_s = sem("pv_s")
        o_hi = sem("o_hi")
        o_lo = sem("o_lo")
        wo_s = sem("wo_s")
        res_s = sem("res_s")
        bn_s = sem("bn_s")
        mv_s = sem("mv_s")
        ve_s = sem("ve_s")
        rstd_s = sem("rstd_s")
        x2_s = sem("x2_s")
        x2t_s = sem("x2t_s")
        x2_hi = sem("x2_hi")
        x2_lo = sem("x2_lo")
        lg_s = sem("lg_s")
        lg_read = sem("lg_read")
        x2_out = [sem(f"x2_out{i}") for i in range(2)]
        rt = sem("rt")
        rt_exp = sem("rt_exp")
        tok0 = sem("tok0")
        tok_zero = sem("tok_zero")
        b_const = sem("b_const")
        counts = sem("counts")
        slots_s = sem("slots_s")
        scat = sem("scat")
        tok_in = sem("tok_in")
        tok_turned = sem("tok_turned")
        idx_s = sem("idx_s")
        fs_in = sem("fs_in")
        f_hi = sem("f_hi")
        f_lo = sem("f_lo")
        sh2_in = sem("sh2_in")
        w2_in = sem("w2_in")
        bx_in = [sem(f"bx_in{i}") for i in range(2)]
        bxg_in = [sem(f"bxg_in{i}") for i in range(2)]
        idxc_s = sem("idxc_s")
        tx_s = sem("tx_s")
        bx_hi = sem("bx_hi")
        bx_lo = sem("bx_lo")
        h_s = sem("h_s")
        sil_s = sem("sil_s")
        g_s = sem("g_s")
        tg_s = sem("tg_s")
        gt_s = sem("gt_s")
        eo_s = sem("eo_s")
        ecp_s = sem("ecp_s")
        eo_out = [sem(f"eo_out{i}") for i in range(2)]
        ic_s = sem("ic_s")
        g_in = [sem(f"g_in{i}") for i in range(2)]
        z_in = [sem(f"z_in{i}") for i in range(2)]
        xres_in = sem("xres_in")
        radd_s = sem("radd_s")
        y_s = sem("y_s")
        fbn = sem("fbn")
        fmv = sem("fmv")
        fve = sem("fve")
        frs = sem("frs")
        o_s = sem("o_s")
        o_out = [sem(f"o_out{i}") for i in range(2)]

        turns = {e.engine: sem(f"turns{n}") for n, e in enumerate((nc.sync, nc.gpsimd, nc.vector, nc.tensor))}

        block = ctx.enter_context(nc.Block())

        PROJ = ["q0", "z", "k0", "q1", "k1", "v0", "v1"]
        QKV_COLS = {"q0": 0, "k0": H * P, "q1": GRP, "k1": H * P + GRP, "v0": 2 * H * P, "v1": 2 * H * P + GRP}
        PROJ_QK = ["q0", "k0", "q1", "k1"]
        W_LOADS = ["q0", "k0", "q1", "k1", "v0", "v1"]

        def projected(s, name):
            return 7 * s + PROJ.index(name) + 1

        NW = 8

        def in_steps(eng, step):
            for s in range(4):
                step(s, s % 2)
            with eng.Fori(2, NT // 2) as i:
                step(2 * i, 0, middle=True)
                step(2 * i + 1, 1, middle=True)
            step(NT, 0)
            step(NT + 1, 1)
            step(NT + 2, 0)

        def settled(eng):
            eng.sem_inc(turns[eng.engine], 1)

        def stages(s, middle):
            return (middle or s < NT), (middle or 1 <= s <= NT), (middle or 2 <= s <= NT + 1), (middle or s >= 3)

        def kind(q):
            return None if q < 0 or q >= NQ else "ex" if S1 <= q < S1 + NX else "sh"

        def row(q, q0):
            return q - S1 if kind(q0) == "ex" else q if q0 < S1 else q - NX

        def shape_of(q):
            return (kind(q - 1), kind(q), kind(q + 1), kind(q + 2), min(q, 4), q < 2 * E, q < 2 * E - 2, S1 - 4 <= q < S1,
                    max(0, min(q - S1 - NX, 5)))

        def tile_steps(eng, step):
            q = 0
            while q < NQ:
                n = 1
                while q + 2 * n < NQ and all(shape_of(q + k) == shape_of(q + 2 * n + k) for k in range(2)):
                    n += 1
                if n > 1:
                    with eng.Fori(q // 2, q // 2 + n) as i:
                        step(2 * i, q, i)
                        step(2 * i + 1, q + 1, i)
                else:
                    step(q, q, q // 2)
                    step(q + 1, q + 1, q // 2)
                q += 2 * n
            step(NQ, NQ, NQ // 2)

        PAIRS = NT // 2
        FIRST = S1 + NX
        LATER = range(NQ - FIRST - 1, PAIRS + 3)

        M_STEP = 19

        def combining(q0):
            return FIRST + 1 <= q0 < NQ

        def phase_a_over(eng):
            eng.wait_ge(lg_read, NT)
            for q in x2_out:
                eng.wait_ge(q, 16 * NT // 2)

        @block.sync
        def _(sp):
            sp.dma_start(xt[:, 0, :, :], xT[:, 0:P].rearrange("(c p) n -> p c n", p=P)).then_inc(xt_in[0], 16)
            for n in range(NW):
                if n >= 4:
                    sp.wait_ge(w_lo, n - 3)
                if n < 6:
                    c0 = [0, H * P, GRP, H * P + GRP, 2 * H * P, 2 * H * P + GRP][n]
                    src = wqkvT[:, c0:c0 + GRP].rearrange("(c p) n -> p c n", p=P)
                else:
                    src = woT[(n - 6) * HPG * P:(n - 5) * HPG * P, :].rearrange("(c p) n -> p c n", p=P)
                sp.dma_start(stage[n % 4], src).then_inc(w_in[n % 4], 16)

            def step(s, par, middle=False):
                proj_on, attn_on, out_on, route_on = stages(s, middle)
                if middle or s + 1 < NT:
                    if middle or s >= 1:
                        sp.wait_ge(x_lo, s)
                        settled(sp)
                    sp.dma_start(xt[:, 1 - par, :, :],
                                 xT[:, bass.ds((s + 1) * P, P)].rearrange("(c p) n -> p c n", p=P))\
                      .then_inc(xt_in[1 - par], 16)
                if out_on:
                    w = s - 2
                    sp.wait_ge(x2_s, w + 1)
                    settled(sp)
                    sp.dma_start(x2_d[bass.ds(w * P, P), :], xr[:, par, :]).then_inc(x2_out[par], 16)
                if proj_on:
                    if middle or s >= 2:
                        sp.wait_ge(x2_out[par], 16 * (s // 2) if not middle else 8 * (s - par))
                        settled(sp)
                        sp.wait_ge(x2t_s, s - 1)
                        settled(sp)
                    sp.dma_start(xr[:, par, :], x[bass.ds(s * P, P), :]).then_inc(xr_in[par], 16)

            in_steps(sp, step)

            phase_a_over(sp)

            def weights(e, n):
                if not isinstance(n, int) or n > 0:
                    sp.wait_ge(f_lo, n)
                    settled(sp)
                sp.dma_start(fs[:, :, :], w13T[bass.ds(e, 1), :, :].rearrange("a (c p) n -> p (a c) n", p=P))\
                  .then_inc(fs_in, 16)

            def load(q, q0):
                sp.dma_start(bx[:, q0 % 2, :], x2_d[bass.ds(row(q, q0) * P, P), :]).then_inc(bx_in[q0 % 2], 16)

            weights(E, 0)
            load(0, 0)
            load(1, 1)
            sp.dma_start(sh2[:, :, :], w2T[E, :, :].rearrange("(c p) n -> p c n", p=P)).then_inc(sh2_in, 16)
            weights(0, 1)

            def combine(c, c0):
                if c0 >= 3:
                    for k in range(2):
                        sp.wait_ge(o_s, 2 * (c - 3) + k + 1)
                        settled(sp)
                        sp.dma_start(out[bass.ds((2 * (c - 3) + k) * P, P), :], oo[:, k, :]).then_inc(o_out[k], 16)
                if c0 < PAIRS:
                    if c0 >= 2:
                        sp.wait_ge(o_s, 2 * c - 2)
                        settled(sp)
                    sp.dma_start(zl[:, c0 % 2, :, :],
                                 z_d[bass.ds(c * 2 * P, 2 * P), :].rearrange("(t p) n -> p t n", p=P))\
                      .then_inc(z_in[c0 % 2], 16)
                    if c0 >= 1:
                        sp.wait_ge(radd_s, c)
                        settled(sp)
                    sp.dma_start(xres[:, :, :], x2_d[bass.ds(c * 2 * P, 2 * P), :].rearrange("(t p) n -> p t n", p=P))\
                      .then_inc(xres_in, 16)

            def step(q, q0, half):
                par = q0 % 2
                if kind(q0 + 2) == "sh":
                    sp.wait_ge(tx_s, q + 1)
                    settled(sp)
                    load(q + 2, q0 + 2)
                if combining(q0):
                    sp.wait_ge(eo_out[par], 16 * half)
                    sp.wait_ge(eo_out[1 - par], 16 * (half - 1 + par))
                    settled(sp)
                    if q0 == FIRST + 1:
                        sp.wait_ge(eo_s, FIRST)
                    combine(q - FIRST - 1, q0 - FIRST - 1)
                if q0 >= 1:
                    sp.wait_ge(ecp_s, q)
                    settled(sp)
                    dst = eo_d if kind(q0 - 1) == "ex" else z_d
                    sp.dma_start(dst[bass.ds(row(q - 1, q0 - 1) * P, P), :], eo[:, 1 - par, :])\
                      .then_inc(eo_out[1 - par], 16)
                if par and q0 < 2 * E - 2:
                    weights(half + 1, half + 2)
                if q0 == S1 - 3:
                    sp.wait_ge(scat, 16 * NSC)
                    sp.dma_start(tok_t[:, :], tok_d.rearrange("(j p) a -> j (p a)", p=P)).then_inc(tok_in, 16)
                if q0 == S1 - 1:
                    sp.wait_ge(f_lo, E + 1)
                    sp.wait_ge(idx_s, 1)
                    sp.dma_start(w2e[:, :, :, :].rearrange("p e c n -> p (e c) n"),
                                 w2T[0:E, :, :].rearrange("e (c p) n -> p (e c) n", p=P)).then_inc(w2_in, 16)

            tile_steps(sp, step)
            for q in eo_out:
                sp.wait_ge(q, 16 * NQ // 2)
            for c in LATER:
                combine(c, c)
            for q in o_out:
                sp.wait_ge(q, 16 * NT // 2)

        @block.gpsimd
        def _(pool):
            pool.memset(ident[:, :], 0.0).then_inc(ident0, 1)
            pool.memset(nhalf[:, :], -0.5).then_inc(consts, 1)
            pool.memset(mask[:, :, :, :], 0.0).then_inc(ident0, 1)
            pool.memset(prevm[:, :], 0.0).then_inc(ident0, 1)
            pool.memset(flag[:, :], 0.0).then_inc(ident0, 1)
            pool.memset(zt[:, :], 0.0).then_inc(tok0, 1)
            pool.iota(tok[:, :], pattern=[[P, NT]], base=0, channel_multiplier=1,
                      allow_small_or_imprecise_dtypes=True).then_inc(consts, 1)
            pool.wait_ge(tok0, 1)
            pool.dma_start(tok_d.rearrange("(p j) a -> p (j a)", p=P), zt[:, :]).then_inc(tok_zero, 16)
            pool.wait_ge(ident0, 4)
            pool.affine_select(out=ident[:, :], in_=ident[:, :], compare_op=ALU.not_equal, fill=1.0, base=0,
                               pattern=[[-1, P]], channel_multiplier=1).then_inc(consts, 1)
            for slot in range(2):
                m = mask[:, slot, slot, :]
                pool.affine_select(out=m, in_=m, compare_op=ALU.is_ge, fill=-BIG, base=0,
                                   pattern=[[-1, P]], channel_multiplier=1).then_inc(consts, 1)
            for m in (mask[:, 1, 0, :], prevm[:, :]):
                pool.affine_select(out=m, in_=m, compare_op=ALU.is_ge, fill=-BIG, base=0,
                                   pattern=[[1, P]], channel_multiplier=-1).then_inc(consts, 1)
            for i in range(0, NT // 2, BLOCKS // 2):
                pool.memset(flag[:, i:i + 1], -BIG).then_inc(consts, 1)

            def split_x(s, par, first=False):
                pool.wait_ge(xt_in[par], 8 * (s - par) + 16)
                if not first:
                    pool.wait_ge(proj, 7 * (s - 1))
                settled(pool)
                pool.tensor_copy(xh[:, par, :, :], xt[:, par, :, :]).then_inc(x_hi, 1)
                pool.wait_ge(x_hi, s + 1)
                pool.tensor_tensor(xl[:, par, :, :], xt[:, par, :, :], xh[:, par, :, :].bitcast(F32), ALU.subtract)\
                    .then_inc(x_lo, 1)

            def power(n):
                pool.wait_ge(ssmax_s, n + 1)
                pool.wait_ge(scaled, n)
                pool.tensor_tensor(rnorm[:, :], ssmax[:, :], nhalf[:, :], ALU.pow).then_inc(rn_s, 1)

            def power0(n):
                pool.wait_ge(ssmax_s, n + 1)
                pool.tensor_tensor(rnorm[:, :], ssmax[:, :], nhalf[:, :], ALU.pow).then_inc(rn_s, 1)

            def normalise(u, g):
                pool.wait_ge(gs_s, 2 * u + g + 1)
                pool.wait_ge(exp_s, 2 * u + g + 1)
                pool.tensor_tensor(pp[:, g * HPG:(g + 1) * HPG, :], pp[:, g * HPG:(g + 1) * HPG, :],
                                   gs[:, g * HPG:(g + 1) * HPG].unsqueeze(2).to_broadcast([P, HPG, 2 * P]),
                                   ALU.mult).then_inc(pn_s, 1)

            def step(s, par, middle=False):
                proj_on, attn_on, out_on, route_on = stages(s, middle)
                if proj_on:
                    if not middle and s == 0:
                        power0(0)
                    else:
                        power(4 * s)
                if attn_on:
                    normalise(s - 1, 0)
                if out_on:
                    pool.wait_ge(ve_s, s - 1)
                    pool.tensor_tensor(rstd[:, :], vareps[:, :], nhalf[:, 0:1], ALU.pow).then_inc(rstd_s, 1)
                if proj_on:
                    power(4 * s + 1)
                    power(4 * s + 2)
                if attn_on:
                    normalise(s - 1, 1)
                if proj_on:
                    power(4 * s + 3)
                if middle or s + 1 < NT:
                    split_x(s + 1, 1 - par, first=(not middle and s == 0))

            split_x(0, 0, first=True)
            in_steps(pool, step)

            phase_a_over(pool)
            pool.memset(tri[:, :], 1.0).then_inc(b_const, 1)
            pool.memset(ones[:, :], 1.0).then_inc(b_const, 1)
            pool.memset(carry[:, :, :], 1.0).then_inc(b_const, 1)
            pool.iota(rev[:, :, :], pattern=[[0, NT], [-1, E]], base=E, channel_multiplier=0,
                      allow_small_or_imprecise_dtypes=True).then_inc(b_const, 1)
            pool.iota(jx[:, :, :], pattern=[[1, NX], [0, E]], base=0, channel_multiplier=0,
                      allow_small_or_imprecise_dtypes=True).then_inc(b_const, 1)
            pool.wait_ge(b_const, 5)
            pool.affine_select(out=tri[:, :], in_=tri[:, :], compare_op=ALU.is_ge, fill=0.0, base=-1,
                               pattern=[[1, P]], channel_multiplier=-1).then_inc(b_const, 1)
            pool.memset(carry[:, :, 0:1], 0.0).then_inc(b_const, 1)

            pool.wait_ge(tok_zero, 16)
            pool.wait_ge(slots_s, 1)
            for i in range(NT):
                for k in range(2):
                    pool.indirect_dma_start(out=tok_d, out_offset=bass.IndirectOffsetOnAxis(slot_u[:, k, i:i + 1], 0),
                                            in_=tok[:, i:i + 1], in_offset=None).then_inc(scat, 16)

            def gather(q, q0, half):
                par = q0 % 2
                pool.wait_ge(tx_s, q - 1)
                settled(pool)
                pool.tensor_copy(idxc[:, par, :], idx_u[:, bass.ds(row(q, q0), 1)]).then_inc(idxc_s, 1)
                pool.wait_ge(idxc_s, row(q, q0) + 1)
                settled(pool)
                pool.indirect_dma_start(out=bx[:, par, :], out_offset=None, in_=x2_d,
                                        in_offset=bass.IndirectOffsetOnAxis(idxc[:, par, :], 0)).then_inc(bxg_in[par], 16)

            def combine(c, c0):
                b = c0 % 2
                if c0 < PAIRS:
                    if c0 >= 2:
                        pool.wait_ge(y_s, 4 * (c - 1))
                        settled(pool)
                    for k in range(2):
                        for m in range(2):
                            pool.tensor_copy(ic[:, b, 2 * k + m:2 * k + m + 1],
                                             slot_u[:, m, bass.ds(2 * c + k, 1)]).then_inc(ic_s, 1)
                    pool.wait_ge(ic_s, 4 * c + 4)
                    settled(pool)
                    for k in range(2):
                        for m, dst in enumerate((ga, gb)):
                            pool.indirect_dma_start(
                                out=dst[:, b, k, :], out_offset=None, in_=eo_d,
                                in_offset=bass.IndirectOffsetOnAxis(ic[:, b, 2 * k + m:2 * k + m + 1], 0))\
                                .then_inc(g_in[b], 16)
                if 1 <= c0 <= PAIRS:
                    pool.wait_ge(fve, c)
                    pool.tensor_tensor(rs2[:, 1 - b, :], ve2[:, :], nhalf[:, 0:2], ALU.pow).then_inc(frs, 1)
                if c0 < PAIRS:
                    pool.wait_ge(z_in[b], 8 * (c - b) + 16)
                    pool.wait_ge(xres_in, 16 * c + 16)
                    pool.tensor_tensor(zl[:, b, :, :], zl[:, b, :, :], xres[:, :, :], ALU.add).then_inc(radd_s, 1)

            def step(q, q0, half):
                if kind(q0 + 2) == "ex":
                    if q0 + 2 == S1:
                        pool.wait_ge(idx_s, 1)
                    gather(q + 2, q0 + 2, half)
                if combining(q0):
                    if q0 == FIRST + 1:
                        for r in eo_out:
                            pool.wait_ge(r, 16 * FIRST // 2)
                        pool.wait_ge(eo_s, FIRST)
                    combine(q - FIRST - 1, q0 - FIRST - 1)

            tile_steps(pool, step)
            for c in LATER:
                combine(c, c)

        @block.scalar
        def _(act):
            act.dma_start(wgs[:, 0, :, :], wgT.rearrange("(c p) n -> p c n", p=P)).then_inc(small_in, 16)
            act.dma_start(wgs[:, 1, :, :], gateT.rearrange("(c p) n -> p c n", p=P)).then_inc(small_in, 16)
            act.dma_start(bgb[:, :], bg.partition_broadcast(P)).then_inc(small_in, 16)
            act.dma_start(qks[:, :], qs.rearrange("(p a) -> p a", a=1)).then_inc(small_in, 16)
            act.dma_start(ksc[:, :], ks.rearrange("(p a) -> p a", a=1)).then_inc(small_in, 16)
            act.wait_ge(small_in, 80)
            act.activation(wgp[:, :, :, 0, :], wgs[:, :, :, :], ACT.Copy).then_inc(wg_split, 1)
            for n in range(NW):
                act.wait_ge(w_in[n % 4], 16 * (n // 4 + 1))
                if n < 6:
                    c0 = [0, H * P, GRP, H * P + GRP, 2 * H * P, 2 * H * P + GRP][n]
                    dst = wh[:, :, c0:c0 + GRP]
                else:
                    dst = woh[:, (n - 6) * HPG:(n - 5) * HPG, :]
                act.activation(dst, stage[n % 4], ACT.Copy).then_inc(w_hi, 1)

            def squares(s, j, n, first=False):
                act.wait_ge(proj, projected(s, PROJ_QK[j]))
                if not first:
                    act.wait_ge(ss_s, n)
                act.activation(sq[:, :], psA[j % 2][:, :], ACT.Square).then_inc(sq_s, 1)

            def heads_T(u, g, par, middle):
                act.wait_ge(tr_s, 4 * u + 2 * g + 1)
                if middle or u >= 1:
                    act.wait_ge(sim_s, 4 * (u - 1) + 2 * g + 2)
                act.activation(qT[:, g * HPG:(g + 1) * HPG, :], psT[0][:, :], ACT.Copy, scale=qks[:, 0:1])\
                   .then_inc(trev, 1)
                act.wait_ge(tr_s, 4 * u + 2 * g + 2)
                act.activation(kT[:, par, g * HPG:(g + 1) * HPG, :], psT[1][:, :], ACT.Copy).then_inc(trev, 1)

            def exps(u, g):
                act.wait_ge(nmx_s, 2 * u + g + 1)
                for h in range(g * HPG, (g + 1) * HPG):
                    ins = act.activation(pp[:, h, :], pp[:, h, :], ACT.Exp, bias=nmx[:, h:h + 1],
                                         accum_out=esum[:, h:h + 1])
                ins.then_inc(exp_s, 1)

            def p_T(u, g, first):
                for b in range(2):
                    act.wait_ge(pt_s, 4 * u + 2 * g + b + 1)
                    if b == 0 and not first:
                        act.wait_ge(pv_s, 2 * u + g)
                    act.activation(pT[:, 2 * b:2 * b + 2, :], psT[b][:, :], ACT.Copy).then_inc(ptev, 1)

            def o_high(u, g, first):
                act.wait_ge(pv_s, 2 * u + g + 1)
                if not first:
                    act.wait_ge(wo_s, u)
                act.activation(oh[:, g * HPG:(g + 1) * HPG, :], psO[:, :], ACT.Copy).then_inc(o_hi, 1)

            def v_copy(s, g, par, wait):
                act.wait_ge(proj, projected(s, f"v{g}"))
                if wait:
                    act.wait_ge(pv_s, 2 * (s - 1) + g + 1)
                act.activation(vv[:, par, g * HPG:(g + 1) * HPG, :], psA[g][:, :], ACT.Copy)\
                   .then_inc(v_s, 1)

            def step(s, par, middle=False):
                proj_on, attn_on, out_on, route_on = stages(s, middle)
                u, w = s - 1, s - 2
                first = not middle and s == 0
                u_first = not middle and s == 1
                if proj_on:
                    squares(s, 0, 4 * s, first=first)
                if attn_on:
                    heads_T(u, 0, 1 - par, middle)
                if attn_on:
                    exps(u, 0)
                    heads_T(u, 1, 1 - par, middle)
                if proj_on:
                    squares(s, 1, 4 * s + 1)
                    squares(s, 2, 4 * s + 2)
                if attn_on:
                    exps(u, 1)
                if proj_on:
                    squares(s, 3, 4 * s + 3)
                if attn_on:
                    p_T(u, 0, u_first)
                    o_high(u, 0, u_first)
                if proj_on:
                    v_copy(s, 0, par, attn_on)
                if attn_on:
                    p_T(u, 1, False)
                    o_high(u, 1, u_first)
                if out_on:
                    act.wait_ge(x2t_s, w + 1)
                    if middle or w >= 1:
                        act.wait_ge(lg_s, w)
                    act.activation(x2h[:, :, :], psT[0][:, :], ACT.Copy).then_inc(x2_hi, 1)
                if proj_on:
                    v_copy(s, 1, par, attn_on)
                    act.wait_ge(z_read, s + 1)
                    if attn_on:
                        act.wait_ge(gden_s, 2 * s)
                    act.activation(ez[:, :], zb[:, :], ACT.Exp, scale=-1.0).then_inc(ez_s, 1)

            in_steps(act, step)
            phase_a_over(act)

            def split_w(dst, n):
                act.wait_ge(fs_in, 16 * n + 16)
                act.activation(dst, fs[:, :, :], ACT.Copy).then_inc(f_hi, 1)

            def split_x(q, q0):
                par = q0 % 2
                act.wait_ge(tx_s, q + 1)
                if q0 >= 2:
                    act.wait_ge(h_s, q - 1)
                act.activation(bh[:, par, :, :], bank[par][:, :], ACT.Copy).then_inc(bx_hi, 1)

            act.wait_ge(rt, 3)
            act.activation(wide_t[1][:, :, :], wide_t[0][:, :, :], ACT.Exp).then_inc(rt_exp, 1)
            split_w(sh13h[:, :, :], 0)
            split_x(0, 0)

            def step(q, q0, half):
                par = q0 % 2
                if q0 + 1 < NQ:
                    split_x(q + 1, q0 + 1)
                if q0 >= 1:
                    act.wait_ge(tg_s, q)
                    if q0 >= 3:
                        act.wait_ge(eo_s, q - 2)
                    act.activation(gT[:, 1 - par, :, :], bank[4 + 1 - par][:, 0:I], ACT.Copy).then_inc(gt_s, 1)
                if q0 < NQ:
                    act.wait_ge(h_s, q + 1)
                    if q0 >= 2:
                        act.wait_ge(g_s, q - 1)
                    act.activation(sil[:, par, :], bank[2 + par][:, 0:I], ACT.Silu).then_inc(sil_s, 1)
                if q0 >= 1:
                    act.wait_ge(eo_s, q)
                    if q0 >= 3:
                        act.wait_ge(eo_out[1 - par], 16 * (half - 1 + par))
                    act.activation(eo[:, 1 - par, :], bank[6 + 1 - par][:, :], ACT.Copy).then_inc(ecp_s, 1)
                if par and q0 < 2 * E:
                    split_w(w13h[:, bass.ds(half, 1), :, :].rearrange("p a c n -> p (a c) n"), half + 1)

            tile_steps(act, step)

        @block.tensor
        def _(pe):
            pe.wait_ge(consts, 11)

            def project(s, name, par, first, route_on=False):
                b = psA[0 if name in ("q0", "q1", "v0") else 1]
                if name == "q0":
                    pe.wait_ge(x_lo, s + 1)
                    if not first:
                        pe.wait_ge(v_s, 2 * s - 1)
                if name == "k0":
                    pe.wait_ge(z_read, s + 1)
                    if route_on:
                        pe.wait_ge(lg_read, s - 2)
                if name in ("q1", "k1"):
                    pe.wait_ge(scaled, 4 * s + PROJ_QK.index(name) - 1)
                if name in ("v0", "v1"):
                    pe.wait_ge(scaled, 4 * s + 3 + int(name[1]))
                if first:
                    pe.wait_ge(w_lo, W_LOADS.index(name) + 1)
                cols = slice(QKV_COLS[name], QKV_COLS[name] + GRP)
                for c in range(DC):
                    for k, (a, wt) in enumerate(((xh, wh), (xh, wl), (xl, wh))):
                        mm = pe.matmul(b[:, :], a[:, par, c, :], wt[:, c, cols], start=(c == 0 and k == 0),
                                       stop=(c == DC - 1 and k == 2))
                mm.then_inc(proj, 1)

            def gates(s, par, first):
                if first:
                    pe.wait_ge(wg_split, 2)
                else:
                    pe.wait_ge(v_s, 2 * s)
                for c in range(DC):
                    for k, a in enumerate((xh, xl)):
                        mm = pe.matmul(psA[1][:, 0:2 * H], a[:, par, c, :],
                                       wgp[:, 0, c, :, :].rearrange("p a e -> p (a e)"),
                                       start=(c == 0 and k == 0), stop=(c == DC - 1 and k == 1))
                mm.then_inc(proj, 1)

            def router(v, wait_read):
                pe.wait_ge(x2_lo, v + 1)
                if wait_read:
                    pe.wait_ge(v_s, 2 * NT)
                    pe.wait_ge(lg_read, v)
                for c in range(DC):
                    for k, a in enumerate((x2h, x2l)):
                        mm = pe.matmul(psA[1][:, 2 * E:4 * E], a[:, c, :],
                                       wgp[:, 1, c, :, :].rearrange("p a e -> p (a e)"),
                                       start=(c == 0 and k == 0), stop=(c == DC - 1 and k == 1))
                mm.then_inc(lg_s, 1)

            def turn_qk(u, g, first):
                for b in range(2):
                    pe.wait_ge(scaled, 4 * u + 2 * g + b + 1)
                    if g == 1:
                        pe.wait_ge(trev, 4 * u + b + 1)
                    elif b == 0 and first is None:
                        pe.wait_ge(x2_lo, u - 1)
                        pe.wait_ge(ptev, 4 * u)
                    elif not first:
                        pe.wait_ge(ptev, 4 * u)
                    for h in range(HPG):
                        mm = pe.transpose(psT[b][:, h * P:(h + 1) * P], qkn[:, 2 * g + b, h * P:(h + 1) * P],
                                          ident[:, :])
                    mm.then_inc(tr_s, 1)

            def scores(u, g, first):
                pe.wait_ge(trev, 4 * u + 2 * g + 2)
                for b in range(2):
                    if not (first and g == 0):
                        pe.wait_ge(masked, 8 * u + 4 * (g - 1) + 2 * b + 2)
                    for hh in range(2):
                        h = g * HPG + 2 * b + hh
                        mm = pe.matmul(psS[b][:, hh * 2 * P:(hh + 1) * 2 * P], qT[:, h, :], kT[:, :, h, :],
                                       start=True, stop=True)
                    mm.then_inc(sim_s, 1)

            def turn_p(u, g):
                pe.wait_ge(pn_s, 2 * u + g + 1)
                for b in range(2):
                    if g == 0:
                        pe.wait_ge(trev, 4 * u + 3 + b)
                    else:
                        pe.wait_ge(ptev, 4 * u + 1 + b)
                    for hh in range(2):
                        for k in range(2):
                            mm = pe.transpose(psT[b][:, (2 * hh + k) * P:(2 * hh + k + 1) * P],
                                              pp[:, g * HPG + 2 * b + hh, k * P:(k + 1) * P], ident[:, :])
                    mm.then_inc(pt_s, 1)

            def values(u, g, first):
                pe.wait_ge(ptev, 4 * u + 2 * g + 2)
                pe.wait_ge(v_s, 2 * u + g + 1)
                if not (first and g == 0):
                    pe.wait_ge(o_lo, 2 * u + g)
                for hh in range(HPG):
                    for k in range(2):
                        mm = pe.matmul(psO[:, hh * P:(hh + 1) * P], vv[:, k, g * HPG + hh, :],
                                       pT[:, hh, k * P:(k + 1) * P], start=(k == 0), stop=(k == 1))
                mm.then_inc(pv_s, 1)

            def project_out(w, first):
                pe.wait_ge(o_lo, 2 * w + 2)
                if not first:
                    pe.wait_ge(res_s, w)
                else:
                    pe.wait_ge(w_lo, NW)
                for h in range(H):
                    for k, (a, b) in enumerate(((oh, woh), (oh, wol), (ol, woh))):
                        mm = pe.matmul(psY[:, :], a[:, h, :], b[:, h, :], start=(h == 0 and k == 0),
                                       stop=(h == H - 1 and k == 2))
                mm.then_inc(wo_s, 1)

            def turn_x2(w, par):
                pe.wait_ge(x2_s, w + 1)
                for c in range(DC):
                    mm = pe.transpose(psT[0][:, c * P:(c + 1) * P], xr[:, par, c * P:(c + 1) * P], ident[:, :])
                mm.then_inc(x2t_s, 1)

            def step(s, par, middle=False):
                proj_on, attn_on, out_on, route_on = stages(s, middle)
                u, w = s - 1, s - 2
                first = not middle and s == 0
                u_first = not middle and s == 1
                w_first = not middle and s == 2
                if proj_on:
                    project(s, "q0", par, first)
                if attn_on:
                    turn_qk(u, 0, None if (middle or s >= 3) else u_first)
                if proj_on:
                    gates(s, par, first)
                if route_on:
                    router(s - 3, not proj_on)
                if attn_on:
                    scores(u, 0, u_first)
                if out_on:
                    project_out(w, w_first)
                if attn_on:
                    turn_qk(u, 1, u_first)
                if proj_on:
                    project(s, "k0", par, first, route_on)
                if attn_on:
                    scores(u, 1, u_first)
                if proj_on:
                    project(s, "q1", par, first)
                    project(s, "k1", par, first)
                if attn_on:
                    turn_p(u, 0)
                if proj_on:
                    project(s, "v0", par, first)
                if attn_on:
                    values(u, 0, u_first)
                    turn_p(u, 1)
                if proj_on:
                    project(s, "v1", par, first)
                if attn_on:
                    values(u, 1, u_first)
                if out_on:
                    if attn_on:
                        pe.wait_ge(ptev, 4 * u + 4)
                    turn_x2(w, par)

            in_steps(pe, step)

            pe.wait_ge(b_const, 7)
            pe.wait_ge(rt, M_STEP)
            pe.matmul(bank[6][:, 0:NT * E], tri[:, :], wide_t[5][:, :, :].rearrange("p t e -> p (t e)"),
                      start=True, stop=True).then_inc(counts, 1)
            pe.matmul(bank[7][:, 0:NT * E], ones[:, :], wide_t[5][:, :, :].rearrange("p t e -> p (t e)"),
                      start=True, stop=True).then_inc(counts, 1)

            def turn_tokens(q, q0):
                par = q0 % 2
                landed = bxg_in if kind(q0) == "ex" else bx_in
                pe.wait_ge(landed[par], 8 * (row(q, q0) - par) + 16)
                if q0 >= 2:
                    pe.wait_ge(bx_lo, q - 1)
                for c in range(DC):
                    mm = pe.transpose(bank[par][:, c * P:(c + 1) * P], bx[:, par, c * P:(c + 1) * P], ident[:, :])
                mm.then_inc(tx_s, 1)

            def expert_at(j):
                settled(pe)
                return nc.values_load(expert_of[0:1, bass.ds(j, 1)], engines=[mybir.EngineType.PE], min_val=0,
                                      max_val=E - 1, skip_runtime_bounds_check_because="it is a count cut off at E - 1")

            def hidden(q, q0):
                par = q0 % 2
                pe.wait_ge(bx_lo, q + 1)
                if q0 >= 2:
                    pe.wait_ge(g_s, q - 1)
                if q0 == 0:
                    pe.wait_ge(f_lo, 1)
                if q0 == S1:
                    pe.wait_ge(f_lo, U)
                if kind(q0) == "ex":
                    e = expert_at(row(q, q0))
                    hi, lo = (w[:, bass.ds(e, 1), :, :].rearrange("p a c n -> p (a c) n") for w in (w13h, w13l))
                else:
                    hi, lo = sh13h[:, :, :], sh13l[:, :, :]
                for c in range(DC):
                    for k, (a, b) in enumerate(((bh, hi), (bh, lo), (bl, hi))):
                        mm = pe.matmul(bank[2 + par][:, :], a[:, par, c, :], b[:, c, :], start=(c == 0 and k == 0),
                                       stop=(c == DC - 1 and k == 2))
                mm.then_inc(h_s, 1)

            def turn_g(q, q0):
                par = q0 % 2
                pe.wait_ge(g_s, q + 1)
                if q0 >= 2:
                    pe.wait_ge(gt_s, q - 1)
                for m in range(IC):
                    mm = pe.transpose(bank[4 + par][:, m * P:(m + 1) * P], gg[:, par, m * P:(m + 1) * P], ident[:, :])
                mm.then_inc(tg_s, 1)

            def expert_out(q, q0):
                par = q0 % 2
                pe.wait_ge(gt_s, q + 1)
                if q0 >= 2:
                    pe.wait_ge(ecp_s, q - 1)
                if q0 == 0:
                    pe.wait_ge(sh2_in, 16)
                    pe.wait_ge(slots_s, 1)
                if q0 == S1:
                    pe.wait_ge(w2_in, 16)
                if kind(q0) == "ex":
                    w2 = w2e[:, bass.ds(expert_at(row(q, q0)), 1), :, :].rearrange("p a c n -> p (a c) n")
                else:
                    w2 = sh2[:, :, :]
                for m in range(IC):
                    mm = pe.matmul(bank[6 + par][:, :], gT[:, par, m, :], w2[:, m, :], start=(m == 0), stop=(m == IC - 1))
                mm.then_inc(eo_s, 1)

            turn_tokens(0, 0)

            def step(q, q0, half):
                if q0 == S1 - 2:
                    pe.wait_ge(tok_in, 16)
                    pe.wait_ge(gt_s, S1 - 3)
                    pe.transpose(bank[4][:, 256:256 + NX], tok_t[:, :], ident[0:NX, 0:NX]).then_inc(tok_turned, 1)
                if q0 + 1 < NQ:
                    turn_tokens(q + 1, q0 + 1)
                if q0 >= 1:
                    turn_g(q - 1, q0 - 1)
                if q0 < NQ:
                    hidden(q, q0)
                if q0 >= 1:
                    expert_out(q - 1, q0 - 1)

            tile_steps(pe, step)

        @block.vector
        def _(dve):
            dve.wait_ge(small_in, 80)
            dve.wait_ge(wg_split, 1)
            dve.tensor_tensor(wgp[:, :, :, 1, :], wgs[:, :, :, :], wgp[:, :, :, 0, :].bitcast(F32), ALU.subtract)\
               .then_inc(wg_split, 1)
            dve.scalar_tensor_tensor(out=qks[:, :], in0=qks[:, :], scalar=8.0, in1=ksc[:, :],
                                     op0=ALU.mult, op1=ALU.mult).then_inc(qks_s, 1)
            for n in range(NW):
                dve.wait_ge(w_hi, n + 1)
                if n < 6:
                    c0 = [0, H * P, GRP, H * P + GRP, 2 * H * P, 2 * H * P + GRP][n]
                    hi, lo = wh[:, :, c0:c0 + GRP], wl[:, :, c0:c0 + GRP]
                else:
                    hi, lo = (q[:, (n - 6) * HPG:(n - 5) * HPG, :] for q in (woh, wol))
                dve.tensor_tensor(lo, stage[n % 4], hi.bitcast(F32), ALU.subtract).then_inc(w_lo, 1)
            dve.wait_ge(w_lo, NW)
            dve.memset(kT[:, 1, :, :], 0.0).then_inc(kv_clear, 1)
            dve.memset(vv[:, 1, :, :], 0.0).then_inc(kv_clear, 1)
            dve.wait_ge(kv_clear, 2)
            dve.wait_ge(consts, 11)

            def sums(s, j, first=False):
                n = 4 * s + j
                dve.wait_ge(sq_s, n + 1)
                if not first:
                    dve.wait_ge(ssmax_s, n)
                dve.tensor_reduce(ssum[:, :], sq[:, :].rearrange("p (h d) -> p h d", d=P), AX_X, ALU.add)\
                   .then_inc(ss_s, 1)
                dve.wait_ge(ss_s, n + 1)
                if not first:
                    dve.wait_ge(rn_s, n)
                dve.tensor_scalar(ssmax[:, :], ssum[:, :], 1e-24, None, ALU.max).then_inc(ssmax_s, 1)

            def scale(s, j, attn_on):
                n = 4 * s + j
                dve.wait_ge(rn_s, n + 1)
                if attn_on:
                    dve.wait_ge(tr_s, 4 * (s - 1) + j + 1)
                dve.tensor_tensor(qkn[:, j, :].rearrange("p (h d) -> p h d", d=P),
                                  psA[j % 2][:, :].rearrange("p (h d) -> p h d", d=P),
                                  rnorm[:, :].unsqueeze(2).to_broadcast([P, HPG, P]), ALU.mult).then_inc(scaled, 1)

            def mask_max(u, g, upar, first):
                for b in range(2):
                    dve.wait_ge(sim_s, 4 * u + 2 * g + b + 1)
                    if b == 0 and not first:
                        dve.wait_ge(pt_s, 4 * (u - 1) + 2 * g + 2)
                        dve.wait_ge(exp_s, 2 * (u - 1) + g + 1)
                    settled(dve)
                    for hh in range(2):
                        h = g * HPG + 2 * b + hh
                        dve.tensor_tensor_reduce(
                            pp[:, h, :], psS[b][:, hh * 2 * P:(hh + 1) * 2 * P],
                            mask[:, upar, :, :].rearrange("p k j -> p (k j)"), 1.0, -3e38, ALU.add, ALU.max,
                            mx[:, h:h + 1]).then_inc(masked, 1)
                dve.wait_ge(masked, 8 * u + 4 * g + 4)
                dve.tensor_scalar(nmx[:, g * HPG:(g + 1) * HPG], mx[:, g * HPG:(g + 1) * HPG], -1.0, None, ALU.mult)\
                   .then_inc(nmx_s, 1)

            def gate_scale(u, g, first):
                c = slice(g * HPG, (g + 1) * HPG)
                dve.wait_ge(exp_s, 2 * u + g + 1)
                if g == 0:
                    dve.wait_ge(ez_s, u + 1)
                dve.scalar_tensor_tensor(out=gden[:, c], in0=ez[:, c], scalar=1.0, in1=esum[:, c],
                                         op0=ALU.add, op1=ALU.mult).then_inc(gden_s, 1)
                dve.wait_ge(gden_s, 2 * u + g + 1)
                if not first:
                    dve.wait_ge(pn_s, 2 * (u - 1) + g + 1)
                dve.reciprocal(gs[:, c], gden[:, c]).then_inc(gs_s, 1)

            def o_low(u, g):
                dve.wait_ge(o_hi, 2 * u + g + 1)
                dve.tensor_tensor(ol[:, g * HPG:(g + 1) * HPG, :].rearrange("p h d -> p (h d)"), psO[:, :],
                                  oh[:, g * HPG:(g + 1) * HPG, :].rearrange("p h d -> p (h d)").bitcast(F32),
                                  ALU.subtract).then_inc(o_lo, 1)

            def layernorm_stats(src, n, bn, m, v, prev):
                dve.bn_stats(bn6[:, :], src).then_inc(bn, 1)
                dve.wait_ge(bn, n + 1)
                settled(dve)
                dve.bn_aggr(mv[:, :], bn6[:, :]).then_inc(m, 1)
                dve.wait_ge(m, n + 1)
                if prev:
                    dve.wait_ge(prev, n)
                dve.tensor_scalar(vareps[:, :], mv[:, 1:2], EPS, None, ALU.add).then_inc(v, 1)

            def step(s, par, middle=False):
                proj_on, attn_on, out_on, route_on = stages(s, middle)
                u, w = s - 1, s - 2
                first = not middle and s == 0
                u_first = not middle and s == 1
                w_first = not middle and s == 2
                if proj_on:
                    sums(s, 0, first)
                    scale(s, 0, attn_on)
                if route_on:
                    dve.wait_ge(lg_s, s - 2)
                    dve.tensor_copy(logits[:, bass.ds(s - 3, 1), :], psA[1][:, 2 * E:4 * E].unsqueeze(1))\
                       .then_inc(lg_read, 1)
                if proj_on:
                    dve.wait_ge(proj, projected(s, "z"))
                    if not first:
                        dve.wait_ge(ez_s, s)
                    dve.tensor_tensor(zt8[:, :], psA[1][:, 0:H], bgb[:, :], ALU.add).then_inc(z_half, 1)
                    dve.wait_ge(z_half, s + 1)
                    dve.tensor_tensor(zb[:, :], psA[1][:, H:2 * H], zt8[:, :], ALU.add).then_inc(z_read, 1)
                if attn_on:
                    mask_max(u, 0, 1 - par, u_first)
                    gate_scale(u, 0, u_first)
                if out_on:
                    dve.wait_ge(wo_s, w + 1)
                    dve.wait_ge(xr_in[par], 8 * (w - par) + 16)
                    dve.tensor_tensor(xr[:, par, :], psY[:, :], xr[:, par, :], ALU.add).then_inc(res_s, 1)
                    dve.wait_ge(res_s, w + 1)
                    layernorm_stats(xr[:, par, :], w, bn_s, mv_s, ve_s, None if w_first else rstd_s)
                    dve.wait_ge(rstd_s, w + 1)
                    dve.tensor_scalar(xr[:, par, :], xr[:, par, :], mv[:, 0:1], rstd[:, 0:1], ALU.subtract, ALU.mult)\
                       .then_inc(x2_s, 1)
                if proj_on:
                    sums(s, 1)
                if attn_on:
                    mask_max(u, 1, 1 - par, u_first)
                if proj_on:
                    scale(s, 1, attn_on)
                    sums(s, 2)
                    scale(s, 2, attn_on)
                if attn_on:
                    gate_scale(u, 1, u_first)
                if proj_on:
                    sums(s, 3)
                    scale(s, 3, attn_on)
                if attn_on:
                    o_low(u, 0)
                    o_low(u, 1)
                if out_on:
                    dve.wait_ge(x2_hi, w + 1)
                    if not w_first:
                        dve.wait_ge(lg_s, w)
                    dve.tensor_tensor(x2l[:, :, :].rearrange("p c n -> p (c n)"), psT[0][:, :],
                                      x2h[:, :, :].rearrange("p c n -> p (c n)").bitcast(F32), ALU.subtract)\
                       .then_inc(x2_lo, 1)

            in_steps_dve(dve, step, mask, prevm, flag, masked, mask_s)

            phase_a_over(dve)
            dve.wait_ge(b_const, 7)
            zt2 = zt[:, :]
            shifted, scores_e, left, first_e, second_e, both_e, work = (w[:, :, :] for w in wide_t)
            wide = [P, NT, E]
            route_step = [0]

            def chained(ins):
                route_step[0] += 1
                ins.then_inc(rt, 1)
                dve.wait_ge(rt, route_step[0])

            def per_tile(ap):
                return ap.unsqueeze(2).to_broadcast(wide)

            chained(dve.tensor_tensor(shifted, logits[:, :, 0:E], logits[:, :, E:2 * E], ALU.add))
            chained(dve.tensor_reduce(r_m[:, :], shifted, AX_X, ALU.max))
            chained(dve.tensor_tensor(shifted, shifted, per_tile(r_m[:, :]), ALU.subtract))
            dve.wait_ge(rt_exp, 1)
            chained(dve.tensor_reduce(r_m[:, :], scores_e, AX_X, ALU.add))
            chained(dve.reciprocal(r_m[:, :], r_m[:, :]))
            chained(dve.tensor_tensor(scores_e, scores_e, per_tile(r_m[:, :]), ALU.mult))
            chained(dve.tensor_copy(left, scores_e))
            for k, chosen in enumerate((first_e, second_e)):
                chained(dve.tensor_reduce(r_m[:, :], left, AX_X, ALU.max))
                chained(dve.tensor_tensor(work, left, per_tile(r_m[:, :]), ALU.is_equal))
                chained(dve.tensor_tensor(work, work, rev[:, :, :], ALU.mult))
                chained(dve.tensor_reduce(r_m[:, :], work, AX_X, ALU.max))
                chained(dve.tensor_tensor(chosen, rev[:, :, :], per_tile(r_m[:, :]), ALU.is_equal))
                if k == 0:
                    chained(dve.scalar_tensor_tensor(out=left, in0=chosen, scalar=-2.0, in1=scores_e,
                                                     op0=ALU.mult, op1=ALU.add))
            chained(dve.tensor_tensor(both_e, first_e, second_e, ALU.add))
            assert route_step[0] == M_STEP
            for k, chosen in enumerate((first_e, second_e)):
                chained(dve.tensor_tensor(work, scores_e, chosen, ALU.mult))
                chained(dve.tensor_reduce(wt2[:, k, :], work, AX_X, ALU.add))
            dve.wait_ge(counts, 2)
            before = bank[6][:, 0:NT * E].rearrange("p (t e) -> p t e", e=E)
            chained(dve.tensor_copy(tot[:, :, :], bank[7][:, 0:NT * E].rearrange("p (t e) -> p e t", e=E)))

            def flat(t):
                return t[:, :, :].rearrange("p e t -> p (e t)")

            chained(dve.tensor_tensor_scan(flat(inc), flat(carry), flat(tot), 0.0, ALU.mult, ALU.add))
            chained(dve.tensor_tensor(tot[:, :, :], inc[:, :, :], tot[:, :, :], ALU.subtract))
            chained(dve.tensor_scalar(small_i[:, 0, :], inc[:, :, NT - 1], float(P - 1), None, ALU.add))
            chained(dve.tensor_scalar(small_i[:, 1, :], small_i[:, 0, :], 7, None, ALU.arith_shift_right))
            chained(dve.tensor_copy(small[:, 0, :], small_i[:, 1, :]))
            chained(dve.tensor_tensor_scan(small[:, 1, :], ones[:, 0:E], small[:, 0, :], 0.0, ALU.mult, ALU.add))
            chained(dve.tensor_tensor(small[:, 2, :], small[:, 1, :], small[:, 0, :], ALU.subtract))
            chained(dve.tensor_scalar(small[:, 3, :], small[:, 2, :], float(P), None, ALU.mult))
            chained(dve.tensor_tensor(work, before, tot[:, :, :].rearrange("p e t -> p t e"), ALU.add))
            chained(dve.tensor_tensor(work, work, small[:, 3, :].unsqueeze(1).to_broadcast(wide), ALU.add))
            for k, chosen in enumerate((first_e, second_e)):
                chained(dve.tensor_tensor(left, work, chosen, ALU.mult))
                chained(dve.tensor_reduce(r_m[:, :], left, AX_X, ALU.add))
                chained(dve.tensor_copy(slot_u[:, k, :], r_m[:, :]))
            chained(dve.tensor_tensor(jx[:, :, :], jx[:, :, :], small[:, 1, :].unsqueeze(1).to_broadcast([P, NX, E]),
                                      ALU.is_ge))
            dve.wait_ge(tok_zero, 16)
            chained(dve.tensor_reduce(zt2, jx[:, :, :], AX_X, ALU.add))
            chained(dve.tensor_scalar(expert_of[:, :], zt2, float(E - 1), None, ALU.min))
            dve.sem_inc(slots_s, 1)

            def split_w(dst, hi, n):
                dve.wait_ge(f_hi, n + 1)
                dve.tensor_tensor(dst, fs[:, :, :], hi.bitcast(F32), ALU.subtract).then_inc(f_lo, 1)

            def split_x(q, q0):
                par = q0 % 2
                dve.wait_ge(bx_hi, q + 1)
                dve.tensor_tensor(bl[:, par, :, :].rearrange("p c n -> p (c n)"), bank[par][:, :],
                                  bh[:, par, :, :].rearrange("p c n -> p (c n)").bitcast(F32), ALU.subtract)\
                   .then_inc(bx_lo, 1)

            split_w(sh13l[:, :, :], sh13h[:, :, :], 0)
            split_x(0, 0)

            def weighted_sum(c, c0):
                b = c0 % 2
                dve.wait_ge(radd_s, c + 1)
                dve.wait_ge(g_in[b], 32 * (c - b) + 64)
                for m, src in enumerate((ga, gb)):
                    for k in range(2):
                        dve.scalar_tensor_tensor(out=zl[:, b, k, :], in0=src[:, b, k, :],
                                                 scalar=wt2[:, m, bass.ds(2 * c + k, 1)], in1=zl[:, b, k, :],
                                                 op0=ALU.mult, op1=ALU.add).then_inc(y_s, 1)
                    dve.wait_ge(y_s, 4 * c + 2 * m + 2)
                for k in range(2):
                    n = 2 * c + k
                    if c0 > 0 or k > 0:
                        dve.wait_ge(fmv, n)
                    dve.bn_stats(bn6[:, :], zl[:, b, k, :]).then_inc(fbn, 1)
                    dve.wait_ge(fbn, n + 1)
                    settled(dve)
                    dve.bn_aggr(mv2[:, b, k, :], bn6[:, :]).then_inc(fmv, 1)
                dve.wait_ge(fmv, 2 * c + 2)
                if c0 > 0:
                    dve.wait_ge(frs, c)
                dve.tensor_scalar(ve2[:, :], mv2[:, b, :, 1], EPS, None, ALU.add).then_inc(fve, 1)

            def last_norm(c, c0):
                b = c0 % 2
                dve.wait_ge(frs, c + 1)
                for k in range(2):
                    if c0 >= 1:
                        dve.wait_ge(o_out[k], 16 * c)
                    dve.tensor_scalar(oo[:, k, :], zl[:, b, k, :], mv2[:, b, k, 0:1], rs2[:, b, k:k + 1],
                                      ALU.subtract, ALU.mult).then_inc(o_s, 1)

            def combine(c, c0):
                if 2 <= c0 <= PAIRS + 1:
                    last_norm(c - 2, c0 - 2)
                if 1 <= c0 <= PAIRS:
                    weighted_sum(c - 1, c0 - 1)

            def step(q, q0, half):
                par = q0 % 2
                if q0 == S1 - 2:
                    dve.wait_ge(tok_turned, 1)
                    dve.tensor_copy(idx_u[:, :], bank[4][:, 256:256 + NX]).then_inc(idx_s, 1)
                if q0 + 1 < NQ:
                    split_x(q + 1, q0 + 1)
                if q0 < NQ:
                    dve.wait_ge(sil_s, q + 1)
                    if q0 >= 2:
                        dve.wait_ge(tg_s, q - 1)
                    dve.tensor_tensor(gg[:, par, :], bank[2 + par][:, I:2 * I], sil[:, par, :], ALU.mult)\
                       .then_inc(g_s, 1)
                if par and q0 < 2 * E:
                    e = bass.ds(half, 1)
                    split_w(w13l[:, e, :, :].rearrange("p a c n -> p (a c) n"),
                            w13h[:, e, :, :].rearrange("p a c n -> p (a c) n"), half + 1)
                if combining(q0):
                    combine(q - FIRST - 1, q0 - FIRST - 1)

            tile_steps(dve, step)
            for c in LATER:
                combine(c, c)


def in_steps_dve(dve, step, mask, prevm, flag, masked, mask_s):
    def set_mask(s, i, first=False):
        if not first:
            dve.wait_ge(masked, 8 * (s - 1))
        dve.tensor_scalar(mask[:, 0, 1, :], prevm[:, :], flag[:, bass.ds(i, 1)], None, ALU.add).then_inc(mask_s, 1)
        dve.wait_ge(mask_s, i + 1)

    for s in range(4):
        if s % 2:
            set_mask(s, s // 2, first=(s == 1))
        step(s, s % 2)
    with dve.Fori(2, NT // 2) as i:
        step(2 * i, 0, middle=True)
        set_mask(2 * i + 1, i)
        step(2 * i + 1, 1, middle=True)
    step(NT, 0)
    step(NT + 1, 1)
    step(NT + 2, 0)


_INS = ["x", "xT", "wqkvT", "woT", "wgT", "bg", "qs", "ks", "gateT", "w13T", "w2T"]


def kernel(**inputs):
    import numpy as _np
    import concourse.bacc as _bacc
    from concourse import mybir as _mybir
    from concourse.bass_utils import run_bass_kernel_spmd as _run

    a = {k: _np.asarray(v) for k, v in inputs.items()}
    x = a["L0_attn_x"].reshape(T, D)
    w13 = _np.concatenate([_np.concatenate([a["L0_ffn_w1"], a["L0_ffn_w3"]], axis=1),
                           _np.concatenate([a["L0_ffn_ws1"], a["L0_ffn_ws3"]], axis=0)[None]], axis=0)
    w2 = _np.concatenate([a["L0_ffn_w2"], a["L0_ffn_ws2"][None]], axis=0)
    laid = {
        "x": x,
        "xT": _np.pad(x.T, ((0, 0), (0, P))),
        "wqkvT": _np.concatenate([a["L0_attn_Wq"], a["L0_attn_Wkv"]], axis=0).T,
        "woT": a["L0_attn_Wo"].T,
        "wgT": a["L0_attn_Wg"].T,
        "bg": a["L0_attn_bg"],
        "qs": a["L0_attn_q_scale"],
        "ks": a["L0_attn_k_scale"],
        "gateT": a["L0_ffn_gate_w"].T,
        "w13T": w13.transpose(0, 2, 1),
        "w2T": w2.transpose(0, 2, 1),
    }
    nc = _bacc.Bacc("TRN2", target_bir_lowering=False, num_devices=1)
    arrays, args = {}, []
    for name in _INS:
        arr = _np.ascontiguousarray(laid[name])
        arrays[f"in_{name}"] = arr
        args.append(nc.dram_tensor(f"in_{name}", arr.shape, _mybir.dt.from_np(arr.dtype), kind="ExternalInput").ap())
    out = nc.dram_tensor("out_0", (T, D), F32, kind="ExternalOutput").ap()
    block_kernel(nc, *args, out)
    r = _run(nc, [arrays], core_ids=[0])
    return r.results[0]["out_0"].reshape(a["L0_attn_x"].shape)
```

```python
from contextlib import ExitStack

import concourse.bass as bass
from concourse import mybir

ALU = mybir.AluOpType
ACT = mybir.ActivationFunctionType
F32 = mybir.dt.float32
F32R = mybir.dt.float32r
U32 = mybir.dt.uint32
I32 = mybir.dt.int32
AX_X = mybir.AxisListType.X

P = 128
D = 512
DC = D // P
H = 8
T = 4096
NT = T // P
BLOCKS = 8
E = 8
I = 256
IC = I // P
EPS = 1e-5
BIG = 1e38
GRP = 512
HPG = GRP // P
NX = (2 * T + E * (P - 1)) // P
NX += NX % 2
S1 = 22
POOL_SPLITS = 2
NQ = NX + NT
NSC = 2 * NT


def block_kernel(nc, x, xT, wqkvT, woT, wgT, bg, qs, ks, gateT, w13T, w2T, out):
    x2_d = nc.dram_tensor("x2_d", [T, D], F32, kind="Internal").ap()
    slot_d = nc.dram_tensor("slot_d", [NX * P, 2], F32, kind="Internal").ap()
    eo_d = nc.dram_tensor("eo_d", [2 * T + NX * P, D], F32, kind="Internal").ap()
    z_d = nc.dram_tensor("z_d", [T, D], F32, kind="Internal").ap()

    with ExitStack() as ctx:
        def sem(name):
            return ctx.enter_context(nc.semaphore(name))

        def sbuf(stack, name, shape, dt=F32):
            return stack.enter_context(nc.sbuf_tensor(name, shape, dt))

        bank = [ctx.enter_context(nc.psum_tensor(f"bank{i}", [P, GRP], F32)) for i in range(8)]
        psA, psS, psT, psO, psY = bank[0:2], bank[2:4], bank[4:6], bank[6], bank[7]

        ident = sbuf(ctx, "ident", [P, P])
        logits = sbuf(ctx, "logits", [P, NT, 2 * E])
        rstd = sbuf(ctx, "rstd", [P, 1])
        nhalf = sbuf(ctx, "nhalf", [P, HPG])
        bn6 = sbuf(ctx, "bn6", [P, 6])
        mv = sbuf(ctx, "mv", [P, 2])
        vareps = sbuf(ctx, "vareps", [P, 1])
        rec = sbuf(ctx, "rec", [P, NT, 2, 2])
        slot_u = sbuf(ctx, "slot_u", [P, 2, NT], U32)
        idx_u = sbuf(ctx, "idx_u", [P, NX], U32)
        dst_u = sbuf(ctx, "dst_u", [P, NX], U32)
        slot_f = sbuf(ctx, "slot_f", [P, 2, NX])
        slot_w = sbuf(ctx, "slot_w", [P, NX])
        expert_of = sbuf(ctx, "expert_of", [P, NX], I32)

        sa = ExitStack()
        wh = sbuf(sa, "wh", [P, DC, 3 * H * P], F32R)
        wl = sbuf(sa, "wl", [P, DC, 3 * H * P], F32R)
        sw = ExitStack()
        passing = sbuf(sw, "passing", [P, 4, DC, GRP])
        sw.close()
        woh = sbuf(sa, "woh", [P, H, D], F32R)
        wol = sbuf(sa, "wol", [P, H, D], F32R)
        wgs = sbuf(sa, "wgs", [P, 2, DC, E])
        wgp = sbuf(sa, "wgp", [P, 2, DC, 2, E], F32R)
        bgb = sbuf(sa, "bgb", [P, H])
        qks = sbuf(sa, "qks", [P, 1])
        ksc = sbuf(sa, "ksc", [P, 1])
        prevm = sbuf(sa, "prevm", [P, P])
        flag = sbuf(sa, "flag", [P, NT // 2])
        mask = sbuf(sa, "mask", [P, 2, 2, P])
        xt = sbuf(sa, "xt", [P, 2, DC, P])
        xh = sbuf(sa, "xh", [P, 2, DC, P], F32R)
        xl = sbuf(sa, "xl", [P, 2, DC, P], F32R)
        xr = sbuf(sa, "xr", [P, 2, D])
        sq = sbuf(sa, "sq", [P, GRP])
        ssum = sbuf(sa, "ssum", [P, HPG])
        ssmax = sbuf(sa, "ssmax", [P, HPG])
        rnorm = sbuf(sa, "rnorm", [P, HPG])
        qkn = sbuf(sa, "qkn", [P, 4, GRP])
        qT = sbuf(sa, "qT", [P, H, P])
        kT = sbuf(sa, "kT", [P, 2, H, P])
        vv = sbuf(sa, "vv", [P, 2, H, P])
        pp = sbuf(sa, "pp", [P, H, 2 * P])
        mx = sbuf(sa, "mx", [P, H])
        nmx = sbuf(sa, "nmx", [P, H])
        esum = sbuf(sa, "esum", [P, H])
        zt8 = sbuf(sa, "zt8", [P, H])
        zb = sbuf(sa, "zb", [P, H])
        ez = sbuf(sa, "ez", [P, H])
        gden = sbuf(sa, "gden", [P, H])
        gs = sbuf(sa, "gs", [P, H])
        pT = sbuf(sa, "pT", [P, HPG, 2 * P])
        oh = sbuf(sa, "oh", [P, H, P], F32R)
        ol = sbuf(sa, "ol", [P, H, P], F32R)
        x2h = sbuf(sa, "x2h", [P, DC, P], F32R)
        x2l = sbuf(sa, "x2l", [P, DC, P], F32R)
        stage = [pp[:, :, :].rearrange("p h (a c) -> p (h a c)", c=GRP // 2).rearrange("p (c n) -> p c n", n=GRP),
                 kT[:, :, :, :].rearrange("p s h d -> p (s h d)").rearrange("p (c n) -> p c n", n=GRP)]
        stage += [passing[:, i, :, :] for i in range(4)]
        sa.close()

        sb = ExitStack()
        s3 = ExitStack()
        ga = sbuf(s3, "ga", [P, 2, 2, D])
        gb = sbuf(s3, "gb", [P, 2, 2, D])
        zl = sbuf(s3, "zl", [P, 2, 2, D])
        oo = sbuf(s3, "oo", [P, 2, D])
        ve2 = sbuf(s3, "ve2", [P, 2])
        mv2 = sbuf(s3, "mv2", [P, 2, 2, 2])
        rs2 = sbuf(s3, "rs2", [P, 2, 2])
        nm2 = sbuf(s3, "nm2", [P, 2, 2])
        s3.close()
        s1 = ExitStack()
        wide_t = [sbuf(s1, f"r{n}", [P, NT, E]) for n in range(7)]
        r_m = sbuf(s1, "r_m", [P, NT])
        rev = sbuf(s1, "rev", [P, NT, E])
        tri = sbuf(s1, "tri", [P, P])
        ones = sbuf(s1, "ones", [P, P])
        carry = sbuf(s1, "carry", [P, E, NT])
        tot = sbuf(s1, "tot", [P, E, NT])
        inc = sbuf(s1, "inc", [P, E, NT])
        small = sbuf(s1, "small", [P, 6, E])
        small_i = sbuf(s1, "small_i", [P, 2, E], I32)
        jx = sbuf(s1, "jx", [P, NX, E])
        used = 4 * (11 * NT * E + NT + 2 * P + 8 * E + NX * E)
        sbuf(s1, "to_the_last_two_experts", [P, ((E - 2) * IC * GRP * 4 - used) // 4])
        fs = sbuf(s1, "fs", [P, DC, GRP])
        s1.close()
        w2e = sbuf(sb, "w2e", [P, E, IC, GRP])
        sh13h = sbuf(sb, "sh13h", [P, DC, GRP], F32R)
        sh13l = sbuf(sb, "sh13l", [P, DC, GRP], F32R)
        sh2 = sbuf(sb, "sh2", [P, IC, GRP])
        bx = sbuf(sb, "bx", [P, 2, D])
        bh = sbuf(sb, "bh", [P, 2, DC, P], F32R)
        bl = sbuf(sb, "bl", [P, 2, DC, P], F32R)
        gg = sbuf(sb, "gg", [P, 2, I])
        gT = sbuf(sb, "gT", [P, 2, IC, P])
        eo = sbuf(sb, "eo", [P, 2, D])
        idxc = sbuf(sb, "idxc", [P, 2, 1], U32)
        dstc = sbuf(sb, "dstc", [P, 2, 1], U32)
        slot_t = sbuf(sb, "slot_t", [NX, P, 2])
        s4 = ExitStack()
        zs = sbuf(s4, "zs", [P, NT - S1, D])
        s4.close()
        w13h = sbuf(sb, "w13h", [P, E, DC, GRP], F32R)
        w13l = sbuf(sb, "w13l", [P, E, DC, GRP], F32R)
        sb.close()

        wg_in = sem("wg_in")
        small_in = sem("small_in")
        consts = sem("consts")
        kv_clear = sem("kv_clear")
        ident0 = sem("ident0")
        w_in = [sem(f"w_in{i}") for i in range(6)]
        w_hi = sem("w_hi")
        w_lo = sem("w_lo")
        wg_split = sem("wg_split")
        qks_s = sem("qks_s")
        xt_in = [sem(f"xt_in{i}") for i in range(2)]
        xr_in = [sem(f"xr_in{i}") for i in range(2)]
        x_hi = sem("x_hi")
        x_lo = sem("x_lo")
        proj = sem("proj")
        sq_s = sem("sq_s")
        ss_s = sem("ss_s")
        ssmax_s = sem("ssmax_s")
        rn_s = sem("rn_s")
        scaled = sem("scaled")
        z_half = sem("z_half")
        z_read = sem("z_read")
        ez_s = sem("ez_s")
        v_s = sem("v_s")
        tr_s = sem("tr_s")
        trev = sem("trev")
        sim_s = sem("sim_s")
        mask_s = sem("mask_s")
        masked = sem("masked")
        nmx_s = sem("nmx_s")
        exp_s = sem("exp_s")
        gden_s = sem("gden_s")
        gs_s = sem("gs_s")
        pn_s = sem("pn_s")
        pt_s = sem("pt_s")
        ptev = sem("ptev")
        pv_s = sem("pv_s")
        o_hi = sem("o_hi")
        o_lo = sem("o_lo")
        wo_s = sem("wo_s")
        res_s = sem("res_s")
        bn_s = sem("bn_s")
        mv_s = sem("mv_s")
        ve_s = sem("ve_s")
        rstd_s = sem("rstd_s")
        x2_s = sem("x2_s")
        x2t_s = sem("x2t_s")
        x2_hi = sem("x2_hi")
        x2_lo = sem("x2_lo")
        lg_s = sem("lg_s")
        lg_read = sem("lg_read")
        x2_out = [sem(f"x2_out{i}") for i in range(2)]
        rt = sem("rt")
        rt_exp = sem("rt_exp")
        tok0 = sem("tok0")
        tok_zero = sem("tok_zero")
        b_const = sem("b_const")
        counts = sem("counts")
        slots_s = sem("slots_s")
        scat = sem("scat")
        tok_in = sem("tok_in")
        tok_turned = sem("tok_turned")
        idx_s = sem("idx_s")
        fs_in = sem("fs_in")
        f_hi = sem("f_hi")
        f_lo = sem("f_lo")
        sh2_in = sem("sh2_in")
        w2_in = sem("w2_in")
        bx_in = [sem(f"bx_in{i}") for i in range(2)]
        bxg_in = [sem(f"bxg_in{i}") for i in range(2)]
        idxc_s = sem("idxc_s")
        dstc_s = sem("dstc_s")
        tx_s = sem("tx_s")
        bx_hi = sem("bx_hi")
        bx_lo = sem("bx_lo")
        h_s = sem("h_s")
        res_in = [sem(f"res_in{i}") for i in range(2)]
        zs_in = [sem(f"zs_in{i}") for i in range(2)]
        cnt_read = sem("cnt_read")
        sil_s = sem("sil_s")
        g_s = sem("g_s")
        tg_s = sem("tg_s")
        gt_s = sem("gt_s")
        eo_s = sem("eo_s")
        res_s2 = sem("res_s2")
        wres_s = sem("wres_s")
        eo_out = [sem(f"eo_out{i}") for i in range(2)]
        exo_out = [sem(f"exo_out{i}") for i in range(2)]
        g_in = [sem(f"g_in{i}") for i in range(2)]
        z_in = [sem(f"z_in{i}") for i in range(2)]
        y_s = sem("y_s")
        fbn = sem("fbn")
        fmv = sem("fmv")
        fve = sem("fve")
        frs = sem("frs")
        fnm = sem("fnm")
        o_s = sem("o_s")
        o_out = [sem(f"o_out{i}") for i in range(2)]

        turns = {e.engine: sem(f"turns{n}") for n, e in enumerate((nc.sync, nc.gpsimd, nc.vector, nc.tensor))}

        block = ctx.enter_context(nc.Block())

        PROJ = ["q0", "z", "k0", "q1", "k1", "v0", "v1"]
        QKV_COLS = {"q0": 0, "k0": H * P, "q1": GRP, "k1": H * P + GRP, "v0": 2 * H * P, "v1": 2 * H * P + GRP}
        PROJ_QK = ["q0", "k0", "q1", "k1"]
        W_LOADS = ["q0", "k0", "q1", "k1", "v0", "v1"]

        def projected(s, name):
            return 7 * s + PROJ.index(name) + 1

        NW = 8

        def in_steps(eng, step):
            for s in range(4):
                step(s, s % 2)
            with eng.Fori(2, NT // 2) as i:
                step(2 * i, 0, middle=True)
                step(2 * i + 1, 1, middle=True)
            step(NT, 0)
            step(NT + 1, 1)
            step(NT + 2, 0)

        def settled(eng):
            eng.sem_inc(turns[eng.engine], 1)

        def stages(s, middle):
            return (middle or s < NT), (middle or 1 <= s <= NT), (middle or 2 <= s <= NT + 1), (middle or s >= 3)

        def kind(q):
            return None if q < 0 or q >= NQ else "ex" if S1 <= q < S1 + NX else "sh"

        def row(q, q0):
            return q - S1 if kind(q0) == "ex" else q if q0 < S1 else q - NX

        def shape_of(q):
            return ([kind(q + k) for k in range(-4, 4)], min(q, 8), q < 2 * E, q < 2 * E - 2,
                    max(-12, q - S1) if q < S1 else 0, max(0, min(q - S1 - NX, 5)))

        def taken(q, q0):
            return (res_s2 if kind(q0) == "sh" else wres_s), row(q, q0) + 1

        def stored(q, q0):
            return (eo_out if kind(q0) == "sh" else exo_out)[q0 % 2], 8 * (row(q, q0) - q0 % 2) + 16

        def tile_steps(eng, step):
            q = 0
            while q < NQ:
                n = 1
                while q + 2 * n < NQ and all(shape_of(q + k) == shape_of(q + 2 * n + k) for k in range(2)):
                    n += 1
                if n > 1:
                    with eng.Fori(q // 2, q // 2 + n) as i:
                        step(2 * i, q, i)
                        step(2 * i + 1, q + 1, i)
                else:
                    step(q, q, q // 2)
                    step(q + 1, q + 1, q // 2)
                q += 2 * n
            step(NQ, NQ, NQ // 2)

        PAIRS = NT // 2
        FIRST = S1 + NX
        LATER = range(NQ - FIRST - 1, PAIRS + 2)

        SLOT_BANK = 4 + (S1 - 3) % 2
        M_STEP = 19

        ZS_PARTS = ((0, 4), (4, NT - S1))

        def z_of(c, c0):
            return zl[:, c0 % 2, :, :] if c0 < S1 // 2 else zs[:, 2 * c0 - S1:2 * c0 - S1 + 2, :]

        def combining(q0):
            return FIRST + 1 <= q0 < NQ

        def phase_a_over(eng):
            eng.wait_ge(lg_read, NT)
            for q in x2_out:
                eng.wait_ge(q, 16 * NT // 2)

        @block.sync
        def _(sp):
            sp.dma_start(xt[:, 0, :, :], xT[:, 0:P].rearrange("(c p) n -> p c n", p=P)).then_inc(xt_in[0], 16)
            for n in range(NW):
                if n >= 6:
                    sp.wait_ge(w_lo, n - 5)
                if n < 6:
                    c0 = [0, H * P, GRP, H * P + GRP, 2 * H * P, 2 * H * P + GRP][n]
                    src = wqkvT[:, c0:c0 + GRP].rearrange("(c p) n -> p c n", p=P)
                else:
                    src = woT[(n - 6) * HPG * P:(n - 5) * HPG * P, :].rearrange("(c p) n -> p c n", p=P)
                sp.dma_start(stage[n % 6], src).then_inc(w_in[n % 6], 16)

            def weights(e, n, part):
                if part == 0 and not (isinstance(n, int) and n == 0):
                    sp.wait_ge(f_lo, n)
                    settled(sp)
                c = slice(part * DC // 2, (part + 1) * DC // 2)
                src = w13T[bass.ds(e, 1), :, :].rearrange("a (c p) n -> p (a c) n", p=P)
                sp.dma_start(fs[:, c, :], src[:, c, :]).then_inc(fs_in, 16)

            def load(q, q0):
                sp.dma_start(bx[:, q0 % 2, :], x2_d[bass.ds(row(q, q0) * P, P), :]).then_inc(bx_in[q0 % 2], 16)

            def load_residual(q, q0):
                if q0 >= 2:
                    sp.wait_ge(*stored(q - 2, q0 - 2))
                    settled(sp)
                sp.dma_start(eo[:, q0 % 2, :], x2_d[bass.ds(row(q, q0) * P, P), :]).then_inc(res_in[q0 % 2], 16)

            def step(s, par, middle=False):
                proj_on, attn_on, out_on, route_on = stages(s, middle)
                if not middle and s == NT:
                    sp.wait_ge(proj, 7 * NT)
                    sp.wait_ge(x2_out[0], 16)
                    sp.wait_ge(x2_out[1], 16)
                    for part in range(2):
                        weights(E, 0, part)
                    load(0, 0)
                    load(1, 1)
                    load_residual(0, 0)
                    load_residual(1, 1)
                    sp.dma_start(sh2[:, :, :], w2T[E, :, :].rearrange("(c p) n -> p c n", p=P)).then_inc(sh2_in, 16)
                if middle or s + 1 < NT:
                    if middle or s >= 1:
                        sp.wait_ge(x_lo, s)
                        settled(sp)
                    sp.dma_start(xt[:, 1 - par, :, :],
                                 xT[:, bass.ds((s + 1) * P, P)].rearrange("(c p) n -> p c n", p=P))\
                      .then_inc(xt_in[1 - par], 16)
                if out_on:
                    w = s - 2
                    sp.wait_ge(x2_s, w + 1)
                    settled(sp)
                    sp.dma_start(x2_d[bass.ds(w * P, P), :], xr[:, par, :]).then_inc(x2_out[par], 16)
                if proj_on:
                    if middle or s >= 2:
                        sp.wait_ge(x2_out[par], 16 * (s // 2) if not middle else 8 * (s - par))
                        settled(sp)
                        sp.wait_ge(x2t_s, s - 1)
                        settled(sp)
                    sp.dma_start(xr[:, par, :], x[bass.ds(s * P, P), :]).then_inc(xr_in[par], 16)

            in_steps(sp, step)

            phase_a_over(sp)

            for part in range(2):
                weights(0, 1, part)

            def combine(c, c0):
                b = c0 % 2
                if c0 < PAIRS:
                    if c0 >= 2:
                        sp.wait_ge(y_s, 2 * c - 2)
                        settled(sp)
                    for dst, src in ((ga, eo_d), (gb, eo_d[T:2 * T, :])):
                        sp.dma_start(dst[:, b, :, :],
                                     src[bass.ds(c * 2 * P, 2 * P), :].rearrange("(t p) n -> p t n", p=P))\
                          .then_inc(g_in[b], 16)
                if c0 >= 2:
                    for k in range(2):
                        sp.wait_ge(o_s, 2 * (c - 2) + k + 1)
                        settled(sp)
                        sp.dma_start(out[bass.ds((2 * (c - 2) + k) * P, P), :], oo[:, k, :]).then_inc(o_out[k], 16)
                if c0 < S1 // 2:
                    sp.dma_start(zl[:, b, :, :],
                                 z_d[bass.ds(c * 2 * P, 2 * P), :].rearrange("(t p) n -> p t n", p=P))\
                      .then_inc(z_in[b], 16)

            def step(q, q0, half):
                par = q0 % 2
                if kind(q0 + 2) == "sh":
                    sp.wait_ge(tx_s, q + 1)
                    settled(sp)
                    load(q + 2, q0 + 2)
                if par and 2 <= q0 < 2 * E:
                    weights(half, half + 1, 1)
                if 2 <= q0 < S1:
                    load_residual(q, q0)
                if q0 in (FIRST, FIRST + 1):
                    if q0 == FIRST:
                        sp.wait_ge(h_s, FIRST)
                    a, b = ZS_PARTS[q0 - FIRST]
                    sp.dma_start(zs[:, a:b, :], x2_d[(S1 + a) * P:(S1 + b) * P, :].rearrange("(t p) n -> p t n", p=P))\
                      .then_inc(zs_in[q0 - FIRST], 16)
                if not par and 2 <= q0 < 2 * E:
                    weights(half, half + 1, 0)
                if S1 - 9 <= q0 < S1 - 1:
                    e = q0 - (S1 - 9)
                    if e == 0:
                        sp.wait_ge(slots_s, 1)
                    if e == E - 2:
                        sp.wait_ge(f_lo, E + 1)
                    sp.dma_start(w2e[:, e, :, :], w2T[e, :, :].rearrange("(c p) n -> p c n", p=P)).then_inc(w2_in, 16)
                if q0 == FIRST + 1:
                    for i in range(2):
                        sp.wait_ge(exo_out[i], 16 * NX // 2)
                    sp.wait_ge(eo_s, FIRST)
                if combining(q0):
                    assert 2 * (q0 - FIRST) <= S1
                    combine(q - FIRST - 1, q0 - FIRST - 1)
                if 1 <= q0 <= S1:
                    sp.wait_ge(*taken(q - 1, q0 - 1))
                    settled(sp)
                    sp.dma_start(z_d[bass.ds(row(q - 1, q0 - 1) * P, P), :], eo[:, 1 - par, :])\
                      .then_inc(eo_out[1 - par], 16)
                if q0 == S1 - 4:
                    sp.wait_ge(scat, 16 * NSC)
                    sp.dma_start(slot_t[:, :, :], slot_d.rearrange("(j p) a -> j p a", p=P)).then_inc(tok_in, 16)

            tile_steps(sp, step)
            for q in eo_out:
                sp.wait_ge(q, 16 * S1 // 2)
            for c in LATER:
                combine(c, c)
            for q in o_out:
                sp.wait_ge(q, 16 * NT // 2)

        @block.gpsimd
        def _(pool):
            def split_x(s, par, first=False):
                pool.wait_ge(xt_in[par], 8 * (s - par) + 16)
                if not first:
                    pool.wait_ge(proj, 7 * (s - 1))
                settled(pool)
                pool.tensor_copy(xh[:, par, :, :], xt[:, par, :, :]).then_inc(x_hi, 1)
                pool.wait_ge(x_hi, s + 1)
                pool.tensor_tensor(xl[:, par, :, :], xt[:, par, :, :], xh[:, par, :, :].bitcast(F32), ALU.subtract)\
                    .then_inc(x_lo, 1)

            split_x(0, 0, first=True)
            pool.memset(ident[:, :], 0.0).then_inc(ident0, 1)
            pool.memset(nhalf[:, :], -0.5).then_inc(consts, 1)
            pool.memset(mask[:, :, :, :], 0.0).then_inc(ident0, 1)
            pool.memset(prevm[:, :], 0.0).then_inc(ident0, 1)
            pool.memset(flag[:, :], 0.0).then_inc(ident0, 1)
            pool.iota(rec[:, :, :, 0], pattern=[[P, NT], [T, 2]], base=0, channel_multiplier=1,
                      allow_small_or_imprecise_dtypes=True).then_inc(consts, 1)
            empty = slot_f[:, :, :].rearrange("p a j -> p (a j)").rearrange("p (j a) -> p j a", a=2)
            pool.iota(empty[:, :, 0], pattern=[[1, NX]], base=2 * T, channel_multiplier=NX,
                      allow_small_or_imprecise_dtypes=True).then_inc(tok0, 1)
            pool.memset(empty[:, :, 1], 0.0).then_inc(tok0, 1)
            pool.wait_ge(tok0, 2)
            pool.dma_start(slot_d.rearrange("(p j) a -> p j a", p=P), empty).then_inc(tok_zero, 16)
            pool.wait_ge(ident0, 4)
            pool.affine_select(out=ident[:, :], in_=ident[:, :], compare_op=ALU.not_equal, fill=1.0, base=0,
                               pattern=[[-1, P]], channel_multiplier=1).then_inc(consts, 1)
            for slot in range(2):
                m = mask[:, slot, slot, :]
                pool.affine_select(out=m, in_=m, compare_op=ALU.is_ge, fill=-BIG, base=0,
                                   pattern=[[-1, P]], channel_multiplier=1).then_inc(consts, 1)
            for m in (mask[:, 1, 0, :], prevm[:, :]):
                pool.affine_select(out=m, in_=m, compare_op=ALU.is_ge, fill=-BIG, base=0,
                                   pattern=[[1, P]], channel_multiplier=-1).then_inc(consts, 1)
            for i in range(0, NT // 2, BLOCKS // 2):
                pool.memset(flag[:, i:i + 1], -BIG).then_inc(consts, 1)

            def routing_constants():
                pool.wait_ge(proj, 7 * NT)
                pool.memset(tri[:, :], 1.0).then_inc(b_const, 1)
                pool.memset(ones[:, :], 1.0).then_inc(b_const, 1)
                pool.memset(carry[:, :, :], 1.0).then_inc(b_const, 1)
                pool.iota(rev[:, :, :], pattern=[[0, NT], [-1, E]], base=E, channel_multiplier=0,
                          allow_small_or_imprecise_dtypes=True).then_inc(b_const, 1)
                pool.iota(jx[:, :, :], pattern=[[1, NX], [0, E]], base=0, channel_multiplier=0,
                          allow_small_or_imprecise_dtypes=True).then_inc(b_const, 1)
                pool.wait_ge(b_const, 5)
                pool.affine_select(out=tri[:, :], in_=tri[:, :], compare_op=ALU.is_ge, fill=0.0, base=-1,
                                   pattern=[[1, P]], channel_multiplier=-1).then_inc(b_const, 1)
                pool.memset(carry[:, :, 0:1], 0.0).then_inc(b_const, 1)

            def power(n, first=False):
                pool.wait_ge(ssmax_s, n + 1)
                if not first:
                    pool.wait_ge(scaled, n)
                pool.tensor_tensor(rnorm[:, :], ssmax[:, :], nhalf[:, :], ALU.pow).then_inc(rn_s, 1)

            def normalise(u, g):
                pool.wait_ge(gs_s, 2 * u + g + 1)
                pool.wait_ge(exp_s, 2 * u + g + 1)
                pool.tensor_tensor(pp[:, g * HPG:(g + 1) * HPG, :], pp[:, g * HPG:(g + 1) * HPG, :],
                                   gs[:, g * HPG:(g + 1) * HPG].unsqueeze(2).to_broadcast([P, HPG, 2 * P]),
                                   ALU.mult).then_inc(pn_s, 1)

            def step(s, par, middle=False):
                proj_on, attn_on, out_on, route_on = stages(s, middle)
                if proj_on:
                    power(4 * s, first=(not middle and s == 0))
                if attn_on:
                    normalise(s - 1, 0)
                if out_on:
                    pool.wait_ge(ve_s, s - 1)
                    pool.tensor_tensor(rstd[:, :], vareps[:, :], nhalf[:, 0:1], ALU.pow).then_inc(rstd_s, 1)
                if proj_on:
                    power(4 * s + 1)
                    power(4 * s + 2)
                if attn_on:
                    normalise(s - 1, 1)
                if proj_on:
                    power(4 * s + 3)
                if middle or s + 1 < NT:
                    split_x(s + 1, 1 - par, first=(not middle and s == 0))
                if not middle and s == NT:
                    routing_constants()

            in_steps(pool, step)

            phase_a_over(pool)

            def scatter_records():
                pool.wait_ge(tok_zero, 16)
                pool.wait_ge(slots_s, 1)
                for i in range(NT):
                    for k in range(2):
                        pool.indirect_dma_start(out=slot_d,
                                                out_offset=bass.IndirectOffsetOnAxis(slot_u[:, k, i:i + 1], 0),
                                                in_=rec[:, i, k, :], in_offset=None).then_inc(scat, 16)

            def gather(q, q0):
                par = q0 % 2
                pool.wait_ge(tx_s, q - 1)
                settled(pool)
                pool.tensor_copy(idxc[:, par, :], idx_u[:, bass.ds(row(q, q0), 1)]).then_inc(idxc_s, 1)
                pool.wait_ge(idxc_s, row(q, q0) + 1)
                settled(pool)
                pool.indirect_dma_start(out=bx[:, par, :], out_offset=None, in_=x2_d,
                                        in_offset=bass.IndirectOffsetOnAxis(idxc[:, par, :], 0)).then_inc(bxg_in[par], 16)

            def scatter_results(q, q0):
                par = q0 % 2
                if q0 >= S1 + 2:
                    pool.wait_ge(*stored(q - 2, q0 - 2))
                    settled(pool)
                pool.tensor_copy(dstc[:, par, :], dst_u[:, bass.ds(row(q, q0), 1)]).then_inc(dstc_s, 1)
                pool.wait_ge(*taken(q, q0))
                settled(pool)
                pool.wait_ge(dstc_s, row(q, q0) + 1)
                settled(pool)
                pool.indirect_dma_start(out=eo_d, out_offset=bass.IndirectOffsetOnAxis(dstc[:, par, :], 0),
                                        in_=eo[:, par, :], in_offset=None).then_inc(exo_out[par], 16)

            def combine(c, c0):
                if 1 <= c0 <= PAIRS:
                    if c0 >= 3:
                        pool.wait_ge(o_s, 2 * c - 4)
                        settled(pool)
                    pool.wait_ge(fve, c)
                    pool.tensor_tensor(rs2[:, 1 - c0 % 2, :], ve2[:, :], nhalf[:, 0:2], ALU.pow).then_inc(frs, 1)

            def step(q, q0, half):
                if q0 % 2 and q0 < 2 * POOL_SPLITS:
                    e = bass.ds(half, 1)
                    pool.wait_ge(f_hi, half + 2)
                    settled(pool)
                    pool.tensor_tensor(w13l[:, e, :, :].rearrange("p a c n -> p (a c) n"), fs[:, :, :],
                                       w13h[:, e, :, :].rearrange("p a c n -> p (a c) n").bitcast(F32),
                                       ALU.subtract).then_inc(f_lo, 1)
                if q0 == 2 * POOL_SPLITS:
                    scatter_records()
                if kind(q0 + 3) == "ex":
                    if q0 + 3 == S1:
                        pool.wait_ge(idx_s, 1)
                    gather(q + 3, q0 + 3)
                if q0 >= 1 and kind(q0 - 1) == "ex":
                    scatter_results(q - 1, q0 - 1)
                if combining(q0):
                    combine(q - FIRST - 1, q0 - FIRST - 1)

            tile_steps(pool, step)
            for c in LATER:
                combine(c, c)

        @block.scalar
        def _(act):
            act.dma_start(wgs[:, 0, :, :], wgT.rearrange("(c p) n -> p c n", p=P)).then_inc(wg_in, 16)
            act.dma_start(wgs[:, 1, :, :], gateT.rearrange("(c p) n -> p c n", p=P)).then_inc(wg_in, 16)
            act.dma_start(bgb[:, :], bg.partition_broadcast(P)).then_inc(small_in, 16)
            act.dma_start(qks[:, :], qs.rearrange("(p a) -> p a", a=1)).then_inc(small_in, 16)
            act.dma_start(ksc[:, :], ks.rearrange("(p a) -> p a", a=1)).then_inc(small_in, 16)
            def weight_high(n):
                act.wait_ge(w_in[n % 6], 16 * (n // 6 + 1))
                if n < 6:
                    c0 = QKV_COLS[W_LOADS[n]]
                    dst = wh[:, :, c0:c0 + GRP]
                else:
                    act.wait_ge(w_lo, 6)
                    dst = woh[:, (n - 6) * HPG:(n - 5) * HPG, :]
                act.activation(dst, stage[n % 6], ACT.Copy).then_inc(w_hi, 1)

            weight_high(0)
            act.wait_ge(wg_in, 32)
            act.activation(wgp[:, :, :, 0, :], wgs[:, :, :, :], ACT.Copy).then_inc(wg_split, 1)
            weight_high(1)

            def split_w(dst, n):
                act.wait_ge(fs_in, 32 * n + 32)
                act.activation(dst, fs[:, :, :], ACT.Copy).then_inc(f_hi, 1)

            def split_b(q, q0):
                par = q0 % 2
                act.wait_ge(tx_s, q + 1)
                if q0 >= 2:
                    act.wait_ge(h_s, q - 1)
                act.activation(bh[:, par, :, :], bank[par][:, :], ACT.Copy).then_inc(bx_hi, 1)

            def squares(s, j, n, first=False):
                act.wait_ge(proj, projected(s, PROJ_QK[j]))
                if not first:
                    act.wait_ge(ss_s, n)
                act.activation(sq[:, :], psA[j % 2][:, :], ACT.Square).then_inc(sq_s, 1)

            def heads_T(u, g, par, middle):
                act.wait_ge(tr_s, 4 * u + 2 * g + 1)
                if middle or u >= 1:
                    act.wait_ge(sim_s, 4 * (u - 1) + 2 * g + 2)
                act.activation(qT[:, g * HPG:(g + 1) * HPG, :], psT[0][:, :], ACT.Copy, scale=qks[:, 0:1])\
                   .then_inc(trev, 1)
                act.wait_ge(tr_s, 4 * u + 2 * g + 2)
                if not middle and u == 0 and g == 0:
                    act.wait_ge(w_lo, NW)
                act.activation(kT[:, par, g * HPG:(g + 1) * HPG, :], psT[1][:, :], ACT.Copy).then_inc(trev, 1)

            def exps(u, g):
                act.wait_ge(nmx_s, 2 * u + g + 1)
                for h in range(g * HPG, (g + 1) * HPG):
                    ins = act.activation(pp[:, h, :], pp[:, h, :], ACT.Exp, bias=nmx[:, h:h + 1],
                                         accum_out=esum[:, h:h + 1])
                ins.then_inc(exp_s, 1)

            def p_T(u, g, first):
                for b in range(2):
                    act.wait_ge(pt_s, 4 * u + 2 * g + b + 1)
                    if b == 0 and not first:
                        act.wait_ge(pv_s, 2 * u + g)
                    act.activation(pT[:, 2 * b:2 * b + 2, :], psT[b][:, :], ACT.Copy).then_inc(ptev, 1)

            def o_high(u, g, first):
                act.wait_ge(pv_s, 2 * u + g + 1)
                if not first:
                    act.wait_ge(wo_s, u)
                act.activation(oh[:, g * HPG:(g + 1) * HPG, :], psO[:, :], ACT.Copy).then_inc(o_hi, 1)

            def v_copy(s, g, par, wait):
                act.wait_ge(proj, projected(s, f"v{g}"))
                if wait:
                    act.wait_ge(pv_s, 2 * (s - 1) + g + 1)
                act.activation(vv[:, par, g * HPG:(g + 1) * HPG, :], psA[g][:, :], ACT.Copy)\
                   .then_inc(v_s, 1)

            def step(s, par, middle=False):
                proj_on, attn_on, out_on, route_on = stages(s, middle)
                u, w = s - 1, s - 2
                first = not middle and s == 0
                u_first = not middle and s == 1
                if proj_on:
                    squares(s, 0, 4 * s, first=first)
                if first:
                    for n in (2, 3, 4):
                        weight_high(n)
                        squares(0, n - 1, n - 1)
                    for n in (5, 6, 7):
                        weight_high(n)
                    v_copy(0, 0, 0, False)
                if attn_on:
                    heads_T(u, 0, 1 - par, middle)
                if attn_on:
                    exps(u, 0)
                    heads_T(u, 1, 1 - par, middle)
                if proj_on and not first:
                    squares(s, 1, 4 * s + 1)
                    squares(s, 2, 4 * s + 2)
                if attn_on:
                    exps(u, 1)
                if proj_on and not first:
                    squares(s, 3, 4 * s + 3)
                if attn_on:
                    p_T(u, 0, u_first)
                    o_high(u, 0, u_first)
                if proj_on and not first:
                    v_copy(s, 0, par, attn_on)
                if attn_on:
                    p_T(u, 1, False)
                    o_high(u, 1, u_first)
                if not middle and s == NT:
                    split_w(sh13h[:, :, :], 0)
                    split_b(0, 0)
                if out_on:
                    act.wait_ge(x2t_s, w + 1)
                    if middle or w >= 1:
                        act.wait_ge(lg_s, w)
                    act.activation(x2h[:, :, :], psT[0][:, :], ACT.Copy).then_inc(x2_hi, 1)
                if proj_on:
                    v_copy(s, 1, par, attn_on)
                    act.wait_ge(z_read, s + 1)
                    if attn_on:
                        act.wait_ge(gden_s, 2 * s)
                    act.activation(ez[:, :], zb[:, :], ACT.Exp, scale=-1.0).then_inc(ez_s, 1)

            in_steps(act, step)
            phase_a_over(act)

            act.wait_ge(rt, 3)
            act.activation(wide_t[1][:, :, :], wide_t[0][:, :, :], ACT.Exp).then_inc(rt_exp, 1)

            def combine(c, c0):
                if 2 <= c0 <= PAIRS + 1:
                    b = c0 % 2
                    act.wait_ge(fnm, c - 1)
                    for k in range(2):
                        if c0 >= 3:
                            act.wait_ge(o_out[k], 16 * (c - 2))
                        act.activation(oo[:, k, :], z_of(c - 2, c0 - 2)[:, k, :], ACT.Identity, bias=nm2[:, b, k:k + 1],
                                       scale=rs2[:, b, k:k + 1]).then_inc(o_s, 1)

            def step(q, q0, half):
                par = q0 % 2
                if q0 + 1 < NQ:
                    split_b(q + 1, q0 + 1)
                if q0 >= 1:
                    act.wait_ge(tg_s, q)
                    if q0 >= 3:
                        act.wait_ge(eo_s, q - 2)
                    act.activation(gT[:, 1 - par, :, :], bank[4 + 1 - par][:, 0:I], ACT.Copy).then_inc(gt_s, 1)
                if q0 < NQ:
                    act.wait_ge(h_s, q + 1)
                    if q0 >= 2:
                        act.wait_ge(tg_s, q - 1)
                    act.activation(gg[:, par, :], bank[2 + par][:, 0:I], ACT.Silu).then_inc(sil_s, 1)
                if q0 >= 1 and kind(q0 - 1) == "ex":
                    act.wait_ge(eo_s, q)
                    act.wait_ge(*stored(q - 3, q0 - 3))
                    act.activation(eo[:, 1 - par, :], bank[6 + 1 - par][:, :], ACT.Copy,
                                   scale=slot_w[:, bass.ds(row(q - 1, q0 - 1), 1)]).then_inc(wres_s, 1)
                if par and q0 < 2 * E:
                    split_w(w13h[:, bass.ds(half, 1), :, :].rearrange("p a c n -> p (a c) n"), half + 1)
                if combining(q0):
                    combine(q - FIRST - 1, q0 - FIRST - 1)

            tile_steps(act, step)
            for c in LATER:
                combine(c, c)

        @block.tensor
        def _(pe):

            def turn_tokens(q, q0):
                par = q0 % 2
                landed = bxg_in if kind(q0) == "ex" else bx_in
                pe.wait_ge(landed[par], 8 * (row(q, q0) - par) + 16)
                if q0 >= 2:
                    pe.wait_ge(bx_lo, q - 1)
                for c in range(DC):
                    mm = pe.transpose(bank[par][:, c * P:(c + 1) * P], bx[:, par, c * P:(c + 1) * P], ident[:, :])
                mm.then_inc(tx_s, 1)

            def expert_at(j):
                settled(pe)
                return nc.values_load(expert_of[0:1, bass.ds(j, 1)], engines=[mybir.EngineType.PE], min_val=0,
                                      max_val=E - 1, skip_runtime_bounds_check_because="it is a count cut off at E - 1")

            def hidden(q, q0):
                par = q0 % 2
                pe.wait_ge(bx_lo, q + 1)
                if q0 >= 2:
                    pe.wait_ge(g_s, q - 1)
                if q0 == 0:
                    pe.wait_ge(f_lo, 1)
                if q0 == S1:
                    pe.wait_ge(f_lo, E + 1)
                if kind(q0) == "ex":
                    e = expert_at(row(q, q0))
                    hi, lo = (w[:, bass.ds(e, 1), :, :].rearrange("p a c n -> p (a c) n") for w in (w13h, w13l))
                else:
                    hi, lo = sh13h[:, :, :], sh13l[:, :, :]
                for c in range(DC):
                    for k, (a, b) in enumerate(((bh, hi), (bh, lo), (bl, hi))):
                        mm = pe.matmul(bank[2 + par][:, :], a[:, par, c, :], b[:, c, :], start=(c == 0 and k == 0),
                                       stop=(c == DC - 1 and k == 2))
                mm.then_inc(h_s, 1)

            def turn_g(q, q0):
                par = q0 % 2
                pe.wait_ge(g_s, q + 1)
                if q0 >= 2:
                    pe.wait_ge(gt_s, q - 1)
                for m in range(IC):
                    mm = pe.transpose(bank[4 + par][:, m * P:(m + 1) * P], gg[:, par, m * P:(m + 1) * P], ident[:, :])
                mm.then_inc(tg_s, 1)

            def expert_out(q, q0):
                par = q0 % 2
                pe.wait_ge(gt_s, q + 1)
                if q0 >= 2:
                    pe.wait_ge(*taken(q - 2, q0 - 2))
                if q0 == 0:
                    pe.wait_ge(sh2_in, 16)
                if q0 == 1:
                    pe.wait_ge(cnt_read, 1)
                if q0 == S1:
                    pe.wait_ge(w2_in, 16 * E)
                if kind(q0) == "ex":
                    w2 = w2e[:, bass.ds(expert_at(row(q, q0)), 1), :, :].rearrange("p a c n -> p (a c) n")
                else:
                    w2 = sh2[:, :, :]
                for m in range(IC):
                    mm = pe.matmul(bank[6 + par][:, :], gT[:, par, m, :], w2[:, m, :], start=(m == 0), stop=(m == IC - 1))
                mm.then_inc(eo_s, 1)

            def count_choices():
                pe.wait_ge(b_const, 7)
                pe.wait_ge(rt, M_STEP)
                for n, sums in enumerate((tri, ones)):
                    pe.matmul(bank[7][:, n * NT * E:(n + 1) * NT * E], sums[:, :],
                              wide_t[5][:, :, :].rearrange("p t e -> p (t e)"), start=True, stop=True)\
                      .then_inc(counts, 1)

            def project(s, name, par, first, route_on=False):
                b = psA[0 if name in ("q0", "q1", "v0") else 1]
                if name == "q0":
                    pe.wait_ge(x_lo, s + 1)
                    if not first:
                        pe.wait_ge(v_s, 2 * s - 1)
                if name == "k0":
                    pe.wait_ge(z_read, s + 1)
                    if route_on:
                        pe.wait_ge(lg_read, s - 2)
                if name in ("q1", "k1"):
                    pe.wait_ge(scaled, 4 * s + PROJ_QK.index(name) - 1)
                if name in ("v0", "v1"):
                    pe.wait_ge(scaled, 4 * s + 3 + int(name[1]))
                if first:
                    pe.wait_ge(w_lo, W_LOADS.index(name) + 1)
                cols = slice(QKV_COLS[name], QKV_COLS[name] + GRP)
                for c in range(DC):
                    for k, (a, wt) in enumerate(((xh, wh), (xh, wl), (xl, wh))):
                        mm = pe.matmul(b[:, :], a[:, par, c, :], wt[:, c, cols], start=(c == 0 and k == 0),
                                       stop=(c == DC - 1 and k == 2))
                mm.then_inc(proj, 1)

            def gates(s, par, first):
                if first:
                    pe.wait_ge(wg_split, 2)
                else:
                    pe.wait_ge(v_s, 2 * s)
                for c in range(DC):
                    for k, a in enumerate((xh, xl)):
                        mm = pe.matmul(psA[1][:, 0:2 * H], a[:, par, c, :],
                                       wgp[:, 0, c, :, :].rearrange("p a e -> p (a e)"),
                                       start=(c == 0 and k == 0), stop=(c == DC - 1 and k == 1))
                mm.then_inc(proj, 1)

            def router(v, wait_read):
                pe.wait_ge(x2_lo, v + 1)
                if wait_read:
                    pe.wait_ge(v_s, 2 * NT)
                    pe.wait_ge(lg_read, v)
                for c in range(DC):
                    for k, a in enumerate((x2h, x2l)):
                        mm = pe.matmul(psA[1][:, 2 * E:4 * E], a[:, c, :],
                                       wgp[:, 1, c, :, :].rearrange("p a e -> p (a e)"),
                                       start=(c == 0 and k == 0), stop=(c == DC - 1 and k == 1))
                mm.then_inc(lg_s, 1)

            def turn_qk(u, g, first):
                for b in range(2):
                    pe.wait_ge(scaled, 4 * u + 2 * g + b + 1)
                    if g == 1:
                        pe.wait_ge(trev, 4 * u + b + 1)
                    elif b == 0 and first is None:
                        pe.wait_ge(x2_lo, u - 1)
                        pe.wait_ge(ptev, 4 * u)
                    elif not first:
                        pe.wait_ge(ptev, 4 * u)
                    for h in range(HPG):
                        mm = pe.transpose(psT[b][:, h * P:(h + 1) * P], qkn[:, 2 * g + b, h * P:(h + 1) * P],
                                          ident[:, :])
                    mm.then_inc(tr_s, 1)

            def scores(u, g, first):
                pe.wait_ge(trev, 4 * u + 2 * g + 2)
                if first and g == 0:
                    pe.wait_ge(kv_clear, 2)
                for b in range(2):
                    if not (first and g == 0):
                        pe.wait_ge(masked, 8 * u + 4 * (g - 1) + 2 * b + 2)
                    for hh in range(2):
                        h = g * HPG + 2 * b + hh
                        mm = pe.matmul(psS[b][:, hh * 2 * P:(hh + 1) * 2 * P], qT[:, h, :], kT[:, :, h, :],
                                       start=True, stop=True)
                    mm.then_inc(sim_s, 1)

            def turn_p(u, g):
                pe.wait_ge(pn_s, 2 * u + g + 1)
                for b in range(2):
                    if g == 0:
                        pe.wait_ge(trev, 4 * u + 3 + b)
                    else:
                        pe.wait_ge(ptev, 4 * u + 1 + b)
                    for hh in range(2):
                        for k in range(2):
                            mm = pe.transpose(psT[b][:, (2 * hh + k) * P:(2 * hh + k + 1) * P],
                                              pp[:, g * HPG + 2 * b + hh, k * P:(k + 1) * P], ident[:, :])
                    mm.then_inc(pt_s, 1)

            def values(u, g, first):
                pe.wait_ge(ptev, 4 * u + 2 * g + 2)
                pe.wait_ge(v_s, 2 * u + g + 1)
                if not (first and g == 0):
                    pe.wait_ge(o_lo, 2 * u + g)
                for hh in range(HPG):
                    for k in range(2):
                        mm = pe.matmul(psO[:, hh * P:(hh + 1) * P], vv[:, k, g * HPG + hh, :],
                                       pT[:, hh, k * P:(k + 1) * P], start=(k == 0), stop=(k == 1))
                mm.then_inc(pv_s, 1)

            def project_out(w, first):
                pe.wait_ge(o_lo, 2 * w + 2)
                if not first:
                    pe.wait_ge(res_s, w)
                else:
                    pe.wait_ge(w_lo, NW)
                for h in range(H):
                    for k, (a, b) in enumerate(((oh, woh), (oh, wol), (ol, woh))):
                        mm = pe.matmul(psY[:, :], a[:, h, :], b[:, h, :], start=(h == 0 and k == 0),
                                       stop=(h == H - 1 and k == 2))
                mm.then_inc(wo_s, 1)

            def turn_x2(w, par):
                pe.wait_ge(x2_s, w + 1)
                for c in range(DC):
                    mm = pe.transpose(psT[0][:, c * P:(c + 1) * P], xr[:, par, c * P:(c + 1) * P], ident[:, :])
                mm.then_inc(x2t_s, 1)

            def step(s, par, middle=False):
                proj_on, attn_on, out_on, route_on = stages(s, middle)
                u, w = s - 1, s - 2
                first = not middle and s == 0
                u_first = not middle and s == 1
                w_first = not middle and s == 2
                if not middle and s == NT + 1:
                    pe.wait_ge(v_s, 2 * NT)
                    turn_tokens(0, 0)
                if u_first:
                    pe.wait_ge(consts, 11)
                if proj_on:
                    project(s, "q0", par, first)
                if attn_on:
                    turn_qk(u, 0, None if (middle or s >= 3) else u_first)
                if proj_on:
                    gates(s, par, first)
                if route_on:
                    router(s - 3, not proj_on)
                if attn_on:
                    scores(u, 0, u_first)
                if out_on:
                    project_out(w, w_first)
                if not middle and s == NT + 1:
                    pe.wait_ge(masked, 8 * NT)
                    hidden(0, 0)
                if attn_on:
                    turn_qk(u, 1, u_first)
                if proj_on:
                    project(s, "k0", par, first, route_on)
                if attn_on:
                    scores(u, 1, u_first)
                if proj_on:
                    project(s, "q1", par, first)
                    project(s, "k1", par, first)
                if attn_on:
                    turn_p(u, 0)
                if proj_on:
                    project(s, "v0", par, first)
                if attn_on:
                    values(u, 0, u_first)
                    turn_p(u, 1)
                if proj_on:
                    project(s, "v1", par, first)
                if attn_on:
                    values(u, 1, u_first)
                if out_on:
                    if attn_on:
                        pe.wait_ge(ptev, 4 * u + 4)
                    turn_x2(w, par)

            in_steps(pe, step)

            pe.wait_ge(lg_read, NT)
            def step(q, q0, half):
                if q0 == S1 - 3:
                    pe.wait_ge(tok_in, 16)
                    pe.wait_ge(gt_s, S1 - 4)
                    for n in range(2):
                        pe.transpose(bank[SLOT_BANK][:, I + n * NX:I + (n + 1) * NX], slot_t[:, :, n], ident[0:NX, 0:NX])\
                          .then_inc(tok_turned, 1)
                if q0 + 1 < NQ:
                    turn_tokens(q + 1, q0 + 1)
                if q0 >= 1:
                    turn_g(q - 1, q0 - 1)
                if 1 <= q0 < NQ:
                    hidden(q, q0)
                if q0 == 0:
                    count_choices()
                if q0 >= 1:
                    expert_out(q - 1, q0 - 1)

            tile_steps(pe, step)

        @block.vector
        def _(dve):
            dve.memset(vv[:, 1, :, :], 0.0).then_inc(kv_clear, 1)

            def weight_low(n):
                dve.wait_ge(w_hi, n + 1)
                if n < 6:
                    c0 = QKV_COLS[W_LOADS[n]]
                    hi, lo = wh[:, :, c0:c0 + GRP], wl[:, :, c0:c0 + GRP]
                else:
                    hi, lo = (q[:, (n - 6) * HPG:(n - 5) * HPG, :] for q in (woh, wol))
                dve.tensor_tensor(lo, stage[n % 6], hi.bitcast(F32), ALU.subtract).then_inc(w_lo, 1)

            weight_low(0)
            dve.wait_ge(wg_split, 1)
            dve.tensor_tensor(wgp[:, :, :, 1, :], wgs[:, :, :, :], wgp[:, :, :, 0, :].bitcast(F32), ALU.subtract)\
               .then_inc(wg_split, 1)
            weight_low(1)
            dve.wait_ge(small_in, 48)
            dve.scalar_tensor_tensor(out=qks[:, :], in0=qks[:, :], scalar=8.0, in1=ksc[:, :],
                                     op0=ALU.mult, op1=ALU.mult).then_inc(qks_s, 1)

            def split_w(dst, hi, n):
                dve.wait_ge(f_hi, n + 1)
                dve.tensor_tensor(dst, fs[:, :, :], hi.bitcast(F32), ALU.subtract).then_inc(f_lo, 1)

            def split_b(q, q0):
                par = q0 % 2
                dve.wait_ge(bx_hi, q + 1)
                dve.tensor_tensor(bl[:, par, :, :].rearrange("p c n -> p (c n)"), bank[par][:, :],
                                  bh[:, par, :, :].rearrange("p c n -> p (c n)").bitcast(F32), ALU.subtract)\
                   .then_inc(bx_lo, 1)

            def sums(s, j, first=False):
                n = 4 * s + j
                dve.wait_ge(sq_s, n + 1)
                if not first:
                    dve.wait_ge(ssmax_s, n)
                dve.tensor_reduce(ssum[:, :], sq[:, :].rearrange("p (h d) -> p h d", d=P), AX_X, ALU.add)\
                   .then_inc(ss_s, 1)
                dve.wait_ge(ss_s, n + 1)
                if not first:
                    dve.wait_ge(rn_s, n)
                dve.tensor_scalar(ssmax[:, :], ssum[:, :], 1e-24, None, ALU.max).then_inc(ssmax_s, 1)

            def scale(s, j, attn_on):
                n = 4 * s + j
                dve.wait_ge(rn_s, n + 1)
                if attn_on:
                    dve.wait_ge(tr_s, 4 * (s - 1) + j + 1)
                dve.tensor_tensor(qkn[:, j, :].rearrange("p (h d) -> p h d", d=P),
                                  psA[j % 2][:, :].rearrange("p (h d) -> p h d", d=P),
                                  rnorm[:, :].unsqueeze(2).to_broadcast([P, HPG, P]), ALU.mult).then_inc(scaled, 1)

            def mask_max(u, g, upar, first):
                for b in range(2):
                    dve.wait_ge(sim_s, 4 * u + 2 * g + b + 1)
                    if b == 0 and not first:
                        dve.wait_ge(pt_s, 4 * (u - 1) + 2 * g + 2)
                        dve.wait_ge(exp_s, 2 * (u - 1) + g + 1)
                    settled(dve)
                    for hh in range(2):
                        h = g * HPG + 2 * b + hh
                        dve.tensor_tensor_reduce(
                            pp[:, h, :], psS[b][:, hh * 2 * P:(hh + 1) * 2 * P],
                            mask[:, upar, :, :].rearrange("p k j -> p (k j)"), 1.0, -3e38, ALU.add, ALU.max,
                            mx[:, h:h + 1]).then_inc(masked, 1)
                dve.wait_ge(masked, 8 * u + 4 * g + 4)
                dve.tensor_scalar(nmx[:, g * HPG:(g + 1) * HPG], mx[:, g * HPG:(g + 1) * HPG], -1.0, None, ALU.mult)\
                   .then_inc(nmx_s, 1)

            def gate_scale(u, g, first):
                c = slice(g * HPG, (g + 1) * HPG)
                dve.wait_ge(exp_s, 2 * u + g + 1)
                if g == 0:
                    dve.wait_ge(ez_s, u + 1)
                dve.scalar_tensor_tensor(out=gden[:, c], in0=ez[:, c], scalar=1.0, in1=esum[:, c],
                                         op0=ALU.add, op1=ALU.mult).then_inc(gden_s, 1)
                dve.wait_ge(gden_s, 2 * u + g + 1)
                if not first:
                    dve.wait_ge(pn_s, 2 * (u - 1) + g + 1)
                dve.reciprocal(gs[:, c], gden[:, c]).then_inc(gs_s, 1)

            def o_low(u, g):
                dve.wait_ge(o_hi, 2 * u + g + 1)
                dve.tensor_tensor(ol[:, g * HPG:(g + 1) * HPG, :].rearrange("p h d -> p (h d)"), psO[:, :],
                                  oh[:, g * HPG:(g + 1) * HPG, :].rearrange("p h d -> p (h d)").bitcast(F32),
                                  ALU.subtract).then_inc(o_lo, 1)

            def add_gate(s, first=False):
                dve.wait_ge(proj, projected(s, "z"))
                if not first:
                    dve.wait_ge(ez_s, s)
                dve.tensor_tensor(zt8[:, :], psA[1][:, 0:H], bgb[:, :], ALU.add).then_inc(z_half, 1)
                dve.wait_ge(z_half, s + 1)
                dve.tensor_tensor(zb[:, :], psA[1][:, H:2 * H], zt8[:, :], ALU.add).then_inc(z_read, 1)

            def first_tile():
                sums(0, 0, True)
                add_gate(0, True)
                for j in range(4):
                    if j > 0:
                        sums(0, j)
                    weight_low(j + 2)
                    scale(0, j, False)
                weight_low(6)
                weight_low(7)
                dve.wait_ge(w_lo, NW)
                dve.memset(kT[:, 1, :, :], 0.0).then_inc(kv_clear, 1)
                dve.wait_ge(consts, 11)

            def layernorm_stats(src, n, bn, m, v, prev):
                dve.bn_stats(bn6[:, :], src).then_inc(bn, 1)
                dve.wait_ge(bn, n + 1)
                settled(dve)
                dve.bn_aggr(mv[:, :], bn6[:, :]).then_inc(m, 1)
                dve.wait_ge(m, n + 1)
                if prev:
                    dve.wait_ge(prev, n)
                dve.tensor_scalar(vareps[:, :], mv[:, 1:2], EPS, None, ALU.add).then_inc(v, 1)

            def step(s, par, middle=False):
                proj_on, attn_on, out_on, route_on = stages(s, middle)
                u, w = s - 1, s - 2
                first = not middle and s == 0
                u_first = not middle and s == 1
                w_first = not middle and s == 2
                if first:
                    first_tile()
                    return
                if proj_on:
                    sums(s, 0)
                    scale(s, 0, attn_on)
                if route_on:
                    dve.wait_ge(lg_s, s - 2)
                    dve.tensor_copy(logits[:, bass.ds(s - 3, 1), :], psA[1][:, 2 * E:4 * E].unsqueeze(1))\
                       .then_inc(lg_read, 1)
                if proj_on:
                    add_gate(s)
                if attn_on:
                    mask_max(u, 0, 1 - par, u_first)
                    gate_scale(u, 0, u_first)
                if out_on:
                    dve.wait_ge(wo_s, w + 1)
                    dve.wait_ge(xr_in[par], 8 * (w - par) + 16)
                    dve.tensor_tensor(xr[:, par, :], psY[:, :], xr[:, par, :], ALU.add).then_inc(res_s, 1)
                    dve.wait_ge(res_s, w + 1)
                    layernorm_stats(xr[:, par, :], w, bn_s, mv_s, ve_s, None if w_first else rstd_s)
                    dve.wait_ge(rstd_s, w + 1)
                    dve.tensor_scalar(xr[:, par, :], xr[:, par, :], mv[:, 0:1], rstd[:, 0:1], ALU.subtract, ALU.mult)\
                       .then_inc(x2_s, 1)
                if proj_on:
                    sums(s, 1)
                if attn_on:
                    mask_max(u, 1, 1 - par, u_first)
                if proj_on:
                    scale(s, 1, attn_on)
                    sums(s, 2)
                    scale(s, 2, attn_on)
                if attn_on:
                    gate_scale(u, 1, u_first)
                if proj_on:
                    sums(s, 3)
                    scale(s, 3, attn_on)
                if attn_on:
                    o_low(u, 0)
                    o_low(u, 1)
                if out_on:
                    dve.wait_ge(x2_hi, w + 1)
                    if not w_first:
                        dve.wait_ge(lg_s, w)
                    dve.tensor_tensor(x2l[:, :, :].rearrange("p c n -> p (c n)"), psT[0][:, :],
                                      x2h[:, :, :].rearrange("p c n -> p (c n)").bitcast(F32), ALU.subtract)\
                       .then_inc(x2_lo, 1)
                if not middle and s == NT:
                    split_w(sh13l[:, :, :], sh13h[:, :, :], 0)
                    split_b(0, 0)

            in_steps_dve(dve, step, mask, prevm, flag, masked, mask_s)

            phase_a_over(dve)
            dve.wait_ge(b_const, 7)
            shifted, scores_e, left, first_e, second_e, both_e, work = (w[:, :, :] for w in wide_t)
            wide = [P, NT, E]
            route_step = [0]

            def chained(ins):
                route_step[0] += 1
                ins.then_inc(rt, 1)
                dve.wait_ge(rt, route_step[0])

            def per_tile(ap):
                return ap.unsqueeze(2).to_broadcast(wide)

            chained(dve.tensor_tensor(shifted, logits[:, :, 0:E], logits[:, :, E:2 * E], ALU.add))
            chained(dve.tensor_reduce(r_m[:, :], shifted, AX_X, ALU.max))
            chained(dve.tensor_tensor(shifted, shifted, per_tile(r_m[:, :]), ALU.subtract))
            dve.wait_ge(rt_exp, 1)
            chained(dve.tensor_reduce(r_m[:, :], scores_e, AX_X, ALU.add))
            chained(dve.reciprocal(r_m[:, :], r_m[:, :]))
            chained(dve.tensor_tensor(scores_e, scores_e, per_tile(r_m[:, :]), ALU.mult))
            chained(dve.tensor_copy(left, scores_e))
            for k, chosen in enumerate((first_e, second_e)):
                chained(dve.tensor_reduce(r_m[:, :], left, AX_X, ALU.max))
                chained(dve.tensor_tensor(work, left, per_tile(r_m[:, :]), ALU.is_equal))
                chained(dve.tensor_tensor(work, work, rev[:, :, :], ALU.mult))
                chained(dve.tensor_reduce(r_m[:, :], work, AX_X, ALU.max))
                chained(dve.tensor_tensor(chosen, rev[:, :, :], per_tile(r_m[:, :]), ALU.is_equal))
                if k == 0:
                    chained(dve.scalar_tensor_tensor(out=left, in0=chosen, scalar=-2.0, in1=scores_e,
                                                     op0=ALU.mult, op1=ALU.add))
            chained(dve.tensor_tensor(both_e, first_e, second_e, ALU.add))
            assert route_step[0] == M_STEP
            for k, chosen in enumerate((first_e, second_e)):
                chained(dve.tensor_tensor(work, scores_e, chosen, ALU.mult))
                chained(dve.tensor_reduce(rec[:, :, k, 1], work, AX_X, ALU.add))
            before = shifted

            def flat(t):
                return t[:, :, :].rearrange("p e t -> p (e t)")

            def count_runs():
                dve.wait_ge(counts, 2)
                chained(dve.tensor_copy(before, bank[7][:, 0:NT * E].rearrange("p (t e) -> p t e", e=E)))
                chained(dve.tensor_copy(tot[:, :, :], bank[7][:, NT * E:2 * NT * E].rearrange("p (t e) -> p e t", e=E)))
                dve.sem_inc(cnt_read, 1)

                chained(dve.tensor_tensor_scan(flat(inc), flat(carry), flat(tot), 0.0, ALU.mult, ALU.add))
                chained(dve.tensor_tensor(tot[:, :, :], inc[:, :, :], tot[:, :, :], ALU.subtract))

            def place_runs():
                chained(dve.tensor_scalar(small_i[:, 0, :], inc[:, :, NT - 1], float(P - 1), None, ALU.add))
                chained(dve.tensor_scalar(small_i[:, 1, :], small_i[:, 0, :], 7, None, ALU.arith_shift_right))
                chained(dve.tensor_copy(small[:, 0, :], small_i[:, 1, :]))
                chained(dve.tensor_tensor_scan(small[:, 1, :], ones[:, 0:E], small[:, 0, :], 0.0, ALU.mult, ALU.add))
                chained(dve.tensor_tensor(small[:, 2, :], small[:, 1, :], small[:, 0, :], ALU.subtract))
                chained(dve.tensor_scalar(small[:, 3, :], small[:, 2, :], float(P), None, ALU.mult))

            def place_tokens():
                chained(dve.tensor_tensor(work, before, tot[:, :, :].rearrange("p e t -> p t e"), ALU.add))
                chained(dve.tensor_tensor(work, work, small[:, 3, :].unsqueeze(1).to_broadcast(wide), ALU.add))
                for k, chosen in enumerate((first_e, second_e)):
                    chained(dve.tensor_tensor(left, work, chosen, ALU.mult))
                    chained(dve.tensor_reduce(r_m[:, :], left, AX_X, ALU.add))
                    chained(dve.tensor_copy(slot_u[:, k, :], r_m[:, :]))

            def place_experts():
                chained(dve.tensor_tensor(jx[:, :, :], jx[:, :, :], small[:, 1, :].unsqueeze(1).to_broadcast([P, NX, E]),
                                          ALU.is_ge))
                dve.wait_ge(tok_zero, 16)
                chained(dve.tensor_reduce(slot_f[:, 0, :], jx[:, :, :], AX_X, ALU.add))
                chained(dve.tensor_scalar(expert_of[:, :], slot_f[:, 0, :], float(E - 1), None, ALU.min))
                dve.sem_inc(slots_s, 1)

            def slot_contents():
                dve.wait_ge(tok_turned, 2)
                chained(dve.tensor_copy(slot_f[:, 0, :], bank[SLOT_BANK][:, I:I + NX]))
                chained(dve.tensor_copy(slot_w[:, :], bank[SLOT_BANK][:, I + NX:I + 2 * NX]))
                chained(dve.tensor_copy(dst_u[:, :], slot_f[:, 0, :]))
                chained(dve.tensor_scalar(slot_f[:, 1, :], slot_f[:, 0, :], float(T), float(T), ALU.is_ge, ALU.mult))
                chained(dve.tensor_tensor(slot_f[:, 0, :], slot_f[:, 0, :], slot_f[:, 1, :], ALU.subtract))
                chained(dve.tensor_scalar(idx_u[:, :], slot_f[:, 0, :], float(T - 1), None, ALU.min))
                dve.sem_inc(idx_s, 1)

            def total(c, c0):
                b = c0 % 2
                dve.wait_ge(g_in[b], 16 * (c - b) + 32)
                dve.tensor_tensor(ga[:, b, :, :], ga[:, b, :, :], gb[:, b, :, :], ALU.add).then_inc(y_s, 1)
                dve.wait_ge(y_s, 2 * c + 1)
                z = z_of(c, c0)
                if c0 < S1 // 2:
                    dve.wait_ge(z_in[b], 8 * (c - b) + 16)
                else:
                    dve.wait_ge(res_s2, 2 * c + 2)
                dve.tensor_tensor(z, z, ga[:, b, :, :], ALU.add).then_inc(y_s, 1)
                dve.wait_ge(y_s, 2 * c + 2)
                for k in range(2):
                    n = 2 * c + k
                    if c0 > 0 or k > 0:
                        dve.wait_ge(fmv, n)
                    dve.bn_stats(bn6[:, :], z[:, k, :]).then_inc(fbn, 1)
                    dve.wait_ge(fbn, n + 1)
                    settled(dve)
                    dve.bn_aggr(mv2[:, b, k, :], bn6[:, :]).then_inc(fmv, 1)
                dve.wait_ge(fmv, 2 * c + 2)
                if c0 > 0:
                    dve.wait_ge(frs, c)
                dve.tensor_scalar(ve2[:, :], mv2[:, b, :, 1], EPS, None, ALU.add).then_inc(fve, 1)

            def mean_share(c, c0):
                b = c0 % 2
                dve.wait_ge(frs, c + 1)
                if c0 >= 2:
                    dve.wait_ge(o_s, 2 * c - 2)
                dve.scalar_tensor_tensor(out=nm2[:, b, :], in0=mv2[:, b, :, 0], scalar=-1.0, in1=rs2[:, b, :],
                                         op0=ALU.mult, op1=ALU.mult).then_inc(fnm, 1)

            def combine(c, c0):
                if 2 <= c0 <= PAIRS + 1:
                    mean_share(c - 2, c0 - 2)
                if 1 <= c0 <= PAIRS:
                    total(c - 1, c0 - 1)

            def step(q, q0, half):
                par = q0 % 2
                if q0 == S1 - 3:
                    slot_contents()
                if q0 + 1 < NQ:
                    split_b(q + 1, q0 + 1)
                if q0 < NQ:
                    dve.wait_ge(sil_s, q + 1)
                    dve.tensor_tensor(gg[:, par, :], bank[2 + par][:, I:2 * I], gg[:, par, :], ALU.mult)\
                       .then_inc(g_s, 1)
                if q0 == 1:
                    count_runs()
                if q0 == 2:
                    place_runs()
                if q0 == 3:
                    place_tokens()
                if q0 == 4:
                    place_experts()
                if q0 >= 1 and kind(q0 - 1) == "sh":
                    dve.wait_ge(eo_s, q)
                    if q0 <= S1:
                        dve.wait_ge(res_in[1 - par], 8 * (row(q - 1, q0 - 1) - (1 - par)) + 16)
                        on = eo[:, 1 - par:2 - par, :]
                    else:
                        if q0 == FIRST + 1:
                            dve.wait_ge(zs_in[0], 16)
                        if q0 == FIRST + 1 + ZS_PARTS[1][0]:
                            dve.wait_ge(zs_in[1], 16)
                        on = zs[:, bass.ds(q - 1 - FIRST, 1), :]
                    dve.tensor_tensor(on, bank[6 + 1 - par][:, :].unsqueeze(1), on, ALU.add).then_inc(res_s2, 1)
                if par and 2 * POOL_SPLITS < q0 < 2 * E:
                    e = bass.ds(half, 1)
                    split_w(w13l[:, e, :, :].rearrange("p a c n -> p (a c) n"),
                            w13h[:, e, :, :].rearrange("p a c n -> p (a c) n"), half + 1)
                if combining(q0):
                    combine(q - FIRST - 1, q0 - FIRST - 1)

            tile_steps(dve, step)
            for c in LATER:
                combine(c, c)


def in_steps_dve(dve, step, mask, prevm, flag, masked, mask_s):
    def set_mask(s, i, first=False):
        if not first:
            dve.wait_ge(masked, 8 * (s - 1))
        dve.tensor_scalar(mask[:, 0, 1, :], prevm[:, :], flag[:, bass.ds(i, 1)], None, ALU.add).then_inc(mask_s, 1)
        dve.wait_ge(mask_s, i + 1)

    for s in range(4):
        if s % 2:
            set_mask(s, s // 2, first=(s == 1))
        step(s, s % 2)
    with dve.Fori(2, NT // 2) as i:
        step(2 * i, 0, middle=True)
        set_mask(2 * i + 1, i)
        step(2 * i + 1, 1, middle=True)
    step(NT, 0)
    step(NT + 1, 1)
    step(NT + 2, 0)


_INS = ["x", "xT", "wqkvT", "woT", "wgT", "bg", "qs", "ks", "gateT", "w13T", "w2T"]


def kernel(**inputs):
    import numpy as _np
    import concourse.bacc as _bacc
    from concourse import mybir as _mybir
    from concourse.bass_utils import run_bass_kernel_spmd as _run

    a = {k: _np.asarray(v) for k, v in inputs.items()}
    x = a["L0_attn_x"].reshape(T, D)
    w13 = _np.concatenate([_np.concatenate([a["L0_ffn_w1"], a["L0_ffn_w3"]], axis=1),
                           _np.concatenate([a["L0_ffn_ws1"], a["L0_ffn_ws3"]], axis=0)[None]], axis=0)
    w2 = _np.concatenate([a["L0_ffn_w2"], a["L0_ffn_ws2"][None]], axis=0)
    laid = {
        "x": x,
        "xT": _np.pad(x.T, ((0, 0), (0, P))),
        "wqkvT": _np.concatenate([a["L0_attn_Wq"], a["L0_attn_Wkv"]], axis=0).T,
        "woT": a["L0_attn_Wo"].T,
        "wgT": a["L0_attn_Wg"].T,
        "bg": a["L0_attn_bg"],
        "qs": a["L0_attn_q_scale"],
        "ks": a["L0_attn_k_scale"],
        "gateT": a["L0_ffn_gate_w"].T,
        "w13T": w13.transpose(0, 2, 1),
        "w2T": w2.transpose(0, 2, 1),
    }
    nc = _bacc.Bacc("TRN2", target_bir_lowering=False, num_devices=1)
    arrays, args = {}, []
    for name in _INS:
        arr = _np.ascontiguousarray(laid[name])
        arrays[f"in_{name}"] = arr
        args.append(nc.dram_tensor(f"in_{name}", arr.shape, _mybir.dt.from_np(arr.dtype), kind="ExternalInput").ap())
    out = nc.dram_tensor("out_0", (T, D), F32, kind="ExternalOutput").ap()
    block_kernel(nc, *args, out)
    r = _run(nc, [arrays], core_ids=[0])
    return r.results[0]["out_0"].reshape(a["L0_attn_x"].shape)
```
